# Optimizing a Trainium2 kernel written in Bass

```python
import numpy as np
import jax
import jax.numpy as jnp

def _softmax(x, axis=-1):
    return jax.nn.softmax(x, axis=axis)

def _gelu(x):
    return jax.nn.gelu(x, approximate=True)

def _silu(x):
    return jax.nn.silu(x)

def _sigmoid(x):
    return jax.nn.sigmoid(x)

def _layernorm(x, axis=-1, eps=1e-05):
    m = jnp.mean(x, axis=axis, keepdims=True)
    v = jnp.var(x, axis=axis, keepdims=True)
    return (x - m) / jnp.sqrt(v + eps)

def _scatter_add(tgt, idx, src, axis=0):
    return tgt.at[idx].add(src)

def _segment_sum(src, seg, n):
    return jax.ops.segment_sum(src, seg, n)
kernel_name = 'mk_vit_tower_d2_tok_img1024_r4_8d6f5a'

def setup_inputs(seed: int=0):
    np.random.seed(seed)
    _w = jnp.asarray

    def _rec_inputs():
        import jax
        import jax.numpy as jnp
        _rk = jax.random.key(seed)
        x = -0.00016672 + 0.999947 * jax.random.normal(jax.random.fold_in(_rk, 1), (32, 96, 96, 3), jnp.float32)
        return x
    x = _rec_inputs()

    def _L0_tok_setup():
        import jax, jax.numpy as jnp
        import numpy as np
        P = 16
        E = 256

        def patchify(images, patch_size):
            B, H, W, C = images.shape
            hp, wp = (H // patch_size, W // patch_size)
            x = images.reshape(B, hp, patch_size, wp, patch_size, C)
            x = x.transpose(0, 1, 3, 2, 4, 5)
            return x.reshape(B, hp * wp, patch_size * patch_size * C)
        key = jax.random.key(seed)
        k_img, k_w, k_b, k_pos = jax.random.split(key, 4)
        B, H, W, C = (64, 96, 96, 3)
        patch_dim = P * P * C
        patch_count = H // P * (W // P)
        images = jax.random.normal(k_img, (B, H, W, C), dtype=jnp.float32)
        W_proj = jax.random.normal(k_w, (E, patch_dim), dtype=jnp.float32) * patch_dim ** (-0.5)
        b_proj = jax.random.normal(k_b, (E,), dtype=jnp.float32) * 0.02
        pos_emb = jax.random.normal(k_pos, (patch_count, E), dtype=jnp.float32) * 0.02
        return {'images': images, 'W_proj': W_proj, 'b_proj': b_proj, 'pos_emb': pos_emb}
    _L0_tok_all = _L0_tok_setup()
    _L0_tok_in = {k: v for k, v in _L0_tok_all.items() if k in ('W_proj', 'b_proj', 'pos_emb')}
    del _L0_tok_all

    def _L0_attn_setup():
        import jax, jax.numpy as jnp
        import numpy as np
        B, T, D = (2, 512, 256)
        H = 16
        DH = D // H
        EPS = 1e-06

        def _feature_map(x):
            return jax.nn.elu(x) + 1.0
        key = jax.random.key(seed)
        ks = jax.random.split(key, 9)
        s = 0.02
        return {'x': jax.random.normal(ks[0], (B, T, D), dtype=jnp.float32), 'Wq': jax.random.normal(ks[1], (D, D), dtype=jnp.float32) * s, 'bq': jnp.zeros((D,), dtype=jnp.float32), 'Wk': jax.random.normal(ks[2], (D, D), dtype=jnp.float32) * s, 'bk': jnp.zeros((D,), dtype=jnp.float32), 'Wv': jax.random.normal(ks[3], (D, D), dtype=jnp.float32) * s, 'bv': jnp.zeros((D,), dtype=jnp.float32), 'Wo': jax.random.normal(ks[4], (D, D), dtype=jnp.float32) * s, 'bo': jnp.zeros((D,), dtype=jnp.float32)}
    _L0_attn_all = _L0_attn_setup()
    _L0_attn_in = {k: v for k, v in _L0_attn_all.items() if k in ('Wq', 'bq', 'Wk', 'bk', 'Wv', 'bv', 'Wo', 'bo')}
    del _L0_attn_all

    def _L0_ffn_setup():
        import jax, jax.numpy as jnp
        import numpy as np
        B, S, IN, OUT, E, R = (8, 1024, 256, 256, 8, 8)
        LORA_ALPHA = 16
        SCALING = LORA_ALPHA / R
        key = jax.random.key(seed)
        k = jax.random.split(key, 6)
        x = jax.random.normal(k[0], (B, S, IN), dtype=jnp.float32)
        base_w = jax.random.normal(k[1], (OUT, IN), dtype=jnp.float32) * 0.02
        base_b = jnp.zeros((OUT,), dtype=jnp.float32)
        lora_A = jax.random.normal(k[2], (IN, R), dtype=jnp.float32) * 0.02
        lora_B = jax.random.normal(k[3], (E, R, OUT), dtype=jnp.float32) * 0.02
        router_w = jax.random.normal(k[4], (E, IN), dtype=jnp.float32) * 0.02
        router_b = jnp.zeros((E,), dtype=jnp.float32)
        return {'x': x, 'base_w': base_w, 'base_b': base_b, 'lora_A': lora_A, 'lora_B': lora_B, 'router_w': router_w, 'router_b': router_b}
    _L0_ffn_all = _L0_ffn_setup()
    _L0_ffn_in = {k: v for k, v in _L0_ffn_all.items() if k in ('base_w', 'base_b', 'lora_A', 'lora_B', 'router_w', 'router_b')}
    del _L0_ffn_all

    def _L1_attn_setup():
        import jax, jax.numpy as jnp
        import numpy as np
        B, S, D = (4, 512, 256)
        key = jax.random.key(seed)
        k1, k2, k3, k4 = jax.random.split(key, 4)
        x = jax.random.normal(k1, (B, S, D), dtype=jnp.float32)
        Qw = jax.random.normal(k2, (D, D), dtype=jnp.float32) / 40
        Kw = jax.random.normal(k3, (D, D), dtype=jnp.float32) / 40
        Vw = jax.random.normal(k4, (D, D), dtype=jnp.float32) / 40
        return {'x': x, 'Qw': Qw, 'Kw': Kw, 'Vw': Vw}
    _L1_attn_all = _L1_attn_setup()
    _L1_attn_in = {k: v for k, v in _L1_attn_all.items() if k in ('Qw', 'Kw', 'Vw')}
    del _L1_attn_all

    def _L1_ffn_setup():
        import jax, jax.numpy as jnp
        import numpy as np
        DIM = 256

        def _reference_tuple_inner(x, W_r, W_k, W_v, mu_r, mu_k):
            B, T, C = x.shape
            x_prev = jnp.concatenate([jnp.zeros((B, 1, C), x.dtype), x[:, :-1, :]], axis=1)
            xr = mu_r * x + (1.0 - mu_r) * x_prev
            xk = mu_k * x + (1.0 - mu_k) * x_prev
            r = jax.nn.sigmoid(jnp.einsum('btc,dc->btd', xr, W_r))
            k = jnp.einsum('btc,dc->btd', xk, W_k)
            k_act = jnp.square(jax.nn.relu(k))
            out = r * jnp.einsum('btc,dc->btd', k_act, W_v)
            new_state = x[:, -1, :]
            return (out, new_state)
        key = jax.random.key(seed)
        ks = jax.random.split(key, 6)
        B, T, C = (8, 512, DIM)
        x = jax.random.normal(ks[0], (B, T, C), dtype=jnp.float32)
        s = 1.0 / np.sqrt(C)
        W_r = jax.random.uniform(ks[1], (C, C), jnp.float32, -s, s)
        W_k = jax.random.uniform(ks[2], (C, C), jnp.float32, -s, s)
        W_v = jax.random.uniform(ks[3], (C, C), jnp.float32, -s, s)
        mu_r = jax.random.uniform(ks[4], (C,), jnp.float32)
        mu_k = jax.random.uniform(ks[5], (C,), jnp.float32)
        return {'x': x, 'W_r': W_r, 'W_k': W_k, 'W_v': W_v, 'mu_r': mu_r, 'mu_k': mu_k}
    _L1_ffn_all = _L1_ffn_setup()
    _L1_ffn_in = {k: v for k, v in _L1_ffn_all.items() if k in ('W_r', 'W_k', 'W_v', 'mu_r', 'mu_k')}
    del _L1_ffn_all
    return {'x': x, 'L0_tok_W_proj': _L0_tok_in['W_proj'], 'L0_tok_b_proj': _L0_tok_in['b_proj'], 'L0_tok_pos_emb': _L0_tok_in['pos_emb'], 'L0_attn_Wq': _L0_attn_in['Wq'], 'L0_attn_bq': _L0_attn_in['bq'], 'L0_attn_Wk': _L0_attn_in['Wk'], 'L0_attn_bk': _L0_attn_in['bk'], 'L0_attn_Wv': _L0_attn_in['Wv'], 'L0_attn_bv': _L0_attn_in['bv'], 'L0_attn_Wo': _L0_attn_in['Wo'], 'L0_attn_bo': _L0_attn_in['bo'], 'L0_ffn_base_w': _L0_ffn_in['base_w'], 'L0_ffn_base_b': _L0_ffn_in['base_b'], 'L0_ffn_lora_A': _L0_ffn_in['lora_A'], 'L0_ffn_lora_B': _L0_ffn_in['lora_B'], 'L0_ffn_router_w': _L0_ffn_in['router_w'], 'L0_ffn_router_b': _L0_ffn_in['router_b'], 'L1_attn_Qw': _L1_attn_in['Qw'], 'L1_attn_Kw': _L1_attn_in['Kw'], 'L1_attn_Vw': _L1_attn_in['Vw'], 'L1_ffn_W_r': _L1_ffn_in['W_r'], 'L1_ffn_W_k': _L1_ffn_in['W_k'], 'L1_ffn_W_v': _L1_ffn_in['W_v'], 'L1_ffn_mu_r': _L1_ffn_in['mu_r'], 'L1_ffn_mu_k': _L1_ffn_in['mu_k']}

def reference(x, L0_tok_W_proj, L0_tok_b_proj, L0_tok_pos_emb, L0_attn_Wq, L0_attn_bq, L0_attn_Wk, L0_attn_bk, L0_attn_Wv, L0_attn_bv, L0_attn_Wo, L0_attn_bo, L0_ffn_base_w, L0_ffn_base_b, L0_ffn_lora_A, L0_ffn_lora_B, L0_ffn_router_w, L0_ffn_router_b, L1_attn_Qw, L1_attn_Kw, L1_attn_Vw, L1_ffn_W_r, L1_ffn_W_k, L1_ffn_W_v, L1_ffn_mu_r, L1_ffn_mu_k):
    import jax
    import jax.numpy as jnp

    def _L0_tok_ref(images, W_proj, b_proj, pos_emb):
        import jax, jax.numpy as jnp
        import numpy as np
        P = 16
        E = 256

        def patchify(images, patch_size):
            B, H, W, C = images.shape
            hp, wp = (H // patch_size, W // patch_size)
            x = images.reshape(B, hp, patch_size, wp, patch_size, C)
            x = x.transpose(0, 1, 3, 2, 4, 5)
            return x.reshape(B, hp * wp, patch_size * patch_size * C)
        patches = patchify(images, P)
        out = jnp.einsum('bnd,ed->bne', patches, W_proj) + b_proj + pos_emb[None, :, :]
        return out

    def _L0_attn_ref(x, Wq, bq, Wk, bk, Wv, bv, Wo, bo):
        import jax, jax.numpy as jnp
        import numpy as np
        B, T, D = (2, 512, 256)
        H = 16
        DH = D // H
        EPS = 1e-06

        def _feature_map(x):
            return jax.nn.elu(x) + 1.0
        b, t, d = x.shape
        q = (x @ Wq.T + bq).reshape(b, t, H, DH).transpose(0, 2, 1, 3)
        k = (x @ Wk.T + bk).reshape(b, t, H, DH).transpose(0, 2, 1, 3)
        v = (x @ Wv.T + bv).reshape(b, t, H, DH).transpose(0, 2, 1, 3)
        q = _feature_map(q)
        k = _feature_map(k)
        kv = jnp.einsum('bhtd,bhte->bhtde', k, v)
        kv_cum = jnp.cumsum(kv, axis=2)
        numerator = jnp.einsum('bhtd,bhtde->bhte', q, kv_cum)
        k_cum = jnp.cumsum(k, axis=2)
        denominator = jnp.einsum('bhtd,bhtd->bht', q, k_cum)
        denominator = jnp.maximum(denominator, EPS)[..., None]
        out = numerator / denominator
        out = out.transpose(0, 2, 1, 3).reshape(b, t, d)
        return out @ Wo.T + bo

    def _L0_ffn_ref(x, base_w, base_b, lora_A, lora_B, router_w, router_b):
        import jax, jax.numpy as jnp
        import numpy as np
        B, S, IN, OUT, E, R = (8, 1024, 256, 256, 8, 8)
        LORA_ALPHA = 16
        SCALING = LORA_ALPHA / R
        result = jnp.einsum('bsd,od->bso', x, base_w) + base_b
        logits = jnp.einsum('bsd,ed->bse', x, router_w) + router_b
        gating = jax.nn.softmax(logits, axis=-1).astype(jnp.bfloat16)
        mid = jnp.einsum('bsd,dr->bsr', x, lora_A)
        lora_out = jnp.einsum('bsr,erd,bse->bsd', mid, lora_B, gating.astype(jnp.float32))
        return result + lora_out * SCALING

    def _L1_attn_ref(x, Qw, Kw, Vw):
        import jax, jax.numpy as jnp
        import numpy as np
        B, S, D = (4, 512, 256)
        Q = x @ Qw
        K = x @ Kw
        V = x @ Vw
        d = x.shape[-1]
        S_len = x.shape[-2]
        mask = jnp.where(jnp.tril(jnp.ones((S_len, S_len), dtype=x.dtype)) == 0, -jnp.inf, 0.0).astype(x.dtype)
        scores = jnp.einsum('bqd,bkd->bqk', Q, K) / jnp.sqrt(jnp.asarray(d, x.dtype))
        scores = scores + mask
        attn = jax.nn.softmax(scores, axis=-1)
        return jnp.einsum('bqk,bkd->bqd', attn, V)

    def _L1_ffn_ref(x, W_r, W_k, W_v, mu_r, mu_k):
        import jax, jax.numpy as jnp
        import numpy as np
        DIM = 256

        def _reference_tuple_inner(x, W_r, W_k, W_v, mu_r, mu_k):
            B, T, C = x.shape
            x_prev = jnp.concatenate([jnp.zeros((B, 1, C), x.dtype), x[:, :-1, :]], axis=1)
            xr = mu_r * x + (1.0 - mu_r) * x_prev
            xk = mu_k * x + (1.0 - mu_k) * x_prev
            r = jax.nn.sigmoid(jnp.einsum('btc,dc->btd', xr, W_r))
            k = jnp.einsum('btc,dc->btd', xk, W_k)
            k_act = jnp.square(jax.nn.relu(k))
            out = r * jnp.einsum('btc,dc->btd', k_act, W_v)
            new_state = x[:, -1, :]
            return (out, new_state)
        return _reference_tuple_inner(x, W_r, W_k, W_v, mu_r, mu_k)[0]
    h = _L0_tok_ref(x, L0_tok_W_proj, L0_tok_b_proj, L0_tok_pos_emb)
    h = h + _L0_attn_ref(_layernorm(h, axis=-1), L0_attn_Wq, L0_attn_bq, L0_attn_Wk, L0_attn_bk, L0_attn_Wv, L0_attn_bv, L0_attn_Wo, L0_attn_bo)
    h = h + _L0_ffn_ref(_layernorm(h, axis=-1), L0_ffn_base_w, L0_ffn_base_b, L0_ffn_lora_A, L0_ffn_lora_B, L0_ffn_router_w, L0_ffn_router_b)
    h = h + _L1_attn_ref(_layernorm(h, axis=-1), L1_attn_Qw, L1_attn_Kw, L1_attn_Vw)
    h = h + _L1_ffn_ref(_layernorm(h, axis=-1), L1_ffn_W_r, L1_ffn_W_k, L1_ffn_W_v, L1_ffn_mu_r, L1_ffn_mu_k)
    return h

_drawn_inputs = setup_inputs


def setup_inputs(seed=0):
    import zlib

    import numpy as np

    out = dict(_drawn_inputs(seed))
    spreads = {'L0_attn_bq': (0.0, 2.0),
     'L0_attn_bk': (0.0, 2.0),
     'L0_attn_bv': (0.0, 0.1),
     'L0_attn_bo': (0.0, 0.1),
     'L0_ffn_base_b': (0.0, 0.1),
     'L0_ffn_router_b': (0.0, 0.8)}
    factors = {'L0_tok_pos_emb': 2.87,
     'L0_attn_Wq': 183.558,
     'L0_attn_Wk': 102.44,
     'L0_ffn_lora_A': 4.391,
     'L0_ffn_lora_B': 4.49,
     'L0_ffn_router_w': 8.0,
     'L1_attn_Qw': 3.45,
     'L1_attn_Kw': 3.386,
     'L1_ffn_W_r': 3.415,
     'L1_ffn_mu_r': 7.103}
    for name, (base, spread) in spreads.items():
        noise = np.random.default_rng([zlib.crc32(name.encode()), seed]).standard_normal(out[name].shape)
        drawn = base * np.exp(spread * noise) if base else spread * noise
        out[name] = jnp.asarray(drawn.astype(out[name].dtype))
    for name, factor in factors.items():
        out[name] = (out[name] * factor).astype(out[name].dtype)
    return out
```

```python
from contextlib import ExitStack

import concourse.bass as bass
from concourse import mybir

F32 = mybir.dt.float32
BF16 = mybir.dt.bfloat16
ALU = mybir.AluOpType
ACT = mybir.ActivationFunctionType
AX = mybir.AxisListType.X

P = 128
B, HW, C = 32, 96, 3
PATCH = 16
GRID = HW // PATCH
NTOK = GRID * GRID
PD = PATCH * PATCH * C
KC = PD // P
E = 256
KT = E // P
NH, DH = 16, 16
HPT = P // DH
NE, R = 8, 8
LORA_SCALING = 16.0 / R
LN_EPS = 1e-5
DEN_EPS = 1e-6
STEP_IMGS = 8
STEPS = B // STEP_IMGS
STOK = STEP_IMGS * NTOK
IMGS = [3, 3, 2]
U = len(IMGS)
T = [n * NTOK for n in IMGS]
OFF = [0, T[0], T[0] + T[1]]
TMAX = max(T)
NEG = -1e30
FB = 5


def vit_tower_kernel(nc, a):
    out = a["out"].rearrange("b n e -> (b n) e")

    ctx = ExitStack()
    with ctx:
        def sb(name, shape, dt=F32):
            return ctx.enter_context(nc.sbuf_tensor(name, shape, dt))

        def sem(name):
            return ctx.enter_context(nc.semaphore(name))

        bank = [ctx.enter_context(nc.psum_tensor(f"bank{k}", [P, 512], F32)) for k in range(8)]

        names = ["L0_attn_Wk", "L0_attn_Wv", "L0_attn_Wq", "L0_attn_Wo",
                 "L1_attn_Qw", "L1_attn_Kw", "L1_attn_Vw", "L1_ffn_W_r", "L1_ffn_W_k", "L1_ffn_W_v"]
        wpT = sb("wpT", [P, KC, E])
        wT = {n: sb(n + "_T", [P, KT, E]) for n in names}
        NCAT = E + NE + R
        wcat = sb("wcat", [P, KT, NCAT])
        G = sb("G", [P, KT, E])
        loraB = sb("loraB", [P, E])

        ident = sb("ident", [P, P])
        pos = sb("pos", [TMAX, E])
        bproj = sb("bproj", [TMAX, E])
        bv = sb("bv", [TMAX, E])
        bo = sb("bo", [TMAX, E])
        baseb = sb("baseb", [TMAX, E])
        routb = sb("routb", [TMAX, NE])
        bq = sb("bq", [P, KT])
        bk = sb("bk", [P, KT])
        bq1 = sb("bq1", [P, KT])
        bk1 = sb("bk1", [P, KT])
        mur = sb("mur", [P, KT])
        muk = sb("muk", [P, KT])
        mask01 = sb("mask01", [TMAX, TMAX])
        maskadd = sb("maskadd", [TMAX, TMAX])
        headmask = sb("headmask", [P, HPT])
        blockones = sb("blockones", [P, P])
        restart = sb("restart", [P, STOK])
        mhalf = sb("mhalf", [TMAX, 1])

        xT = sb("xT", [P, KC, STOK])
        hF = sb("hF", [TMAX, U, E])
        hbo = sb("hbo", [TMAX, U, E])
        kT = sb("kT", [P, KT, STOK])
        qT = sb("qT", [P, KT, STOK])
        qexp = sb("qexp", [P, KT, HPT, STOK])
        vpad = sb("vpad", [TMAX, U, NH // 2, 2, 2, DH])
        kcum = sb("kcum", [P, KT, STOK])
        kmin = kcum
        qk = sb("qk", [P, KT, STOK])
        qmin = qk
        rden = sb("rden", [P, KT, STOK])
        S = sb("S", [TMAX, U, NH, TMAX])
        attnT = sb("attnT", [P, U, KT, TMAX])
        hB = sb("hB", [TMAX, U, E])
        hbb = sb("hbb", [TMAX, U, E])
        logit = sb("logit", [TMAX, U, NE])
        lmax = sb("lmax", [TMAX, U])
        lsub = sb("lsub", [TMAX, U, NE])
        lexp = sb("lexp", [TMAX, U, NE])
        lsum = sb("lsum", [TMAX, U])
        lrec = sb("lrec", [TMAX, U])
        gate = sb("gate", [TMAX, U, NE], BF16)
        mid = sb("mid", [TMAX, U, R])
        z = sb("z", [TMAX, U, P])
        zT = sb("zT", [P, U, TMAX])
        at = sb("at", [P, U, KT, TMAX])
        v1 = sb("v1", [TMAX, U, E])
        sm = sb("sm", [TMAX, U, TMAX])
        smax = sb("smax", [TMAX, U])
        nmax = sb("nmax", [TMAX, U])
        prob = sb("prob", [TMAX, U, TMAX])
        psm = sb("psm", [TMAX, U])
        prec = sb("prec", [TMAX, U])
        probT = sb("probT", [TMAX, U, TMAX])
        xs = sb("xs", [P, U, KT, 3, NTOK + 1])
        xd = sb("xd", [P, U, KT, TMAX])
        xr = sb("xr", [P, U, KT, TMAX])
        xk = sb("xk", [P, U, KT, TMAX])
        rt = sb("rt", [TMAX, U, E])
        kact = sb("kact", [P, U, KT, TMAX])
        o_sb = sb("o_sb", [TMAX, U, E])

        xn_back = sb("xn_back", [TMAX, U, E])
        xnT_back = sb("xnT_back", [P, KT, STOK])

        class LN:
            def __init__(self, n):
                self.st = sb(f"ln{n}_st", [TMAX, U, 6])
                self.mv = sb(f"ln{n}_mv", [TMAX, U, 2])
                self.ve = sb(f"ln{n}_ve", [TMAX, U])
                self.rs = sb(f"ln{n}_rs", [TMAX, U])
                self.xn = xn_back if n else sb("xn_front", [TMAX, U, E])
                self.xnT = xnT_back if n else sb("xnT_front", [P, KT, STOK])
                self.stats_done = sem(f"ln{n}_stats_done")
                self.var_done = sem(f"ln{n}_var_done")
                self.eps_added = sem(f"ln{n}_eps_added")
                self.rstd_done = sem(f"ln{n}_rstd_done")
                self.xn_done = sem(f"ln{n}_xn_done")
                self.turned = sem(f"ln{n}_turned")
                self.xnT_ready = sem(f"ln{n}_xnT_ready")

        ln = [LN(n) for n in range(4)]

        s = {n: sem(n) for n in [
            "wp_loaded", "cat_loaded", "lora_loaded", "pos_loaded", "rows_loaded", "vecs_loaded",
            "const_step", "ident_ready", "masks_ready", "zeros_ready", "pos_ready", "bias1_ready",
            "g_mm", "g_ready",
            "tok_mm", "hF_ready", "k_mm", "k_min", "k_exp", "kT_ready",
            "q_mm", "q_min", "q_exp", "qT_ready", "v_mm", "vpad_ready", "qexp_ready", "kcum_ready",
            "qk_ready", "den_mm", "den_floor", "rden_ready", "s_mm", "s_masked", "av_mm", "attnT_ready",
            "wo_mm", "hbo_ready", "h1_ready",
            "ffn_mm", "logit_ready", "lmax_ready", "lsub_ready", "lexp_ready", "lrec_ready", "gate_ready",
            "mid_ready", "z_ready", "hbb_ready", "h2a_ready", "z_turned", "zT_ready", "lora_mm", "h2_ready",
            "atv_mm", "at_ready", "v1_ready", "sc_mm", "sm_ready", "smax_ready", "nmax_ready", "prob_ready",
            "prob_turned", "probT_ready", "pv_mm", "prec_ready", "h3_ready", "xd_ready", "xr_ready",
            "xk_ready", "rk_mm", "rt_ready", "krelu_ready", "kact_ready", "kv_mm", "rkv_ready", "out_ready",
        ]}
        w_loaded = {n: sem(n + "_loaded") for n in names}
        x_loaded = [sem(f"x_loaded{u}") for u in range(U)]
        out_stored = [sem(f"out_stored{u}") for u in range(U)]

        TOK_BANK, LN0_BANK = [0, 1, 2], [3, 0, 1]

        def tr(n, u):
            b = LN0_BANK[u] if n == 0 else FB + u
            return bank[b][:, 0:KT * T[u]].rearrange("p (k t) -> p k t", k=KT)

        block = ctx.enter_context(nc.Block())

        PROLOGUE = ["F_patch", "F_ln", "W_G", "F_qkv", "F_scores", "F_wo"]
        BODY = ["F_patch", "B_ln1", "F_ln", "B_ffn", "B_lora", "F_qkv", "B_ln2", "B_atv", "B_scores",
                "F_scores", "B_pv", "B_ln3", "B_ffn1", "B_out", "F_wo"]
        EPILOGUE = [n for n in BODY if n[0] == "B"]

        def run(eng, steps):
            for name in PROLOGUE:
                if name in steps:
                    steps[name](0)
            with eng.Fori(1, STEPS) as i:
                for name in BODY:
                    if name in steps:
                        steps[name](i if name[0] == "F" else i - 1)
            for name in EPILOGUE:
                if name in steps:
                    steps[name](STEPS - 1)

        @block.sync
        def _(sp):
            def load_x(i, u):
                sp.dma_start(xT[:, :, OFF[u]:OFF[u] + T[u]],
                             a["x"][bass.ds(i * P, P), :, OFF[u]:OFF[u] + T[u]]).then_inc(x_loaded[u], 16)

            def load_w(n, dst, signal):
                sp.dma_start(dst, a[n].rearrange("(t p) n -> p t n", p=P)).then_inc(signal, 16)

            load_w("L0_tok_W_proj", wpT[:, :, :], s["wp_loaded"])
            for u in range(U):
                load_x(0, u)
            for n in names[:4]:
                load_w(n, wT[n][:, :, :], w_loaded[n])
            load_w("L0_ffn_cat", wcat[:, :, :], s["cat_loaded"])
            sp.dma_start(loraB[0:NE * R, :], a["L0_ffn_lora_B"]).then_inc(s["lora_loaded"], 16)
            for n in names[4:]:
                load_w(n, wT[n][:, :, :], w_loaded[n])

            def store(i):
                for u in range(U):
                    sp.wait_ge(s["out_ready"], U * i + u + 1)
                    sp.dma_start(out[bass.ds(i * STOK + OFF[u], T[u]), :],
                                 o_sb[0:T[u], u, :]).then_inc(out_stored[u], 16)

            def fetch(i):
                for u in range(U):
                    sp.wait_ge(s["tok_mm"], U * (i - 1) + u + 1)
                    load_x(i, u)

            fetch(1)
            with sp.Fori(1, STEPS - 1) as i:
                fetch(i + 1)
                store(i - 1)
            store(STEPS - 2)
            store(STEPS - 1)
            for u in range(U):
                sp.wait_ge(out_stored[u], 16 * STEPS + 1)

        @block.gpsimd
        def _(pool):
            def row(dst, n):
                v = a[n].rearrange("(o n) -> o n", o=1)
                pool.dma_start(dst, v.to_broadcast([TMAX, v.shape[1]])).then_inc(s["rows_loaded"], 16)

            nc.gpsimd.memset(ident[:, :], 0.0).then_inc(s["const_step"], 1)
            pool.wait_ge(s["const_step"], 1)
            nc.gpsimd.affine_select(ident[:, :], ident[:, :], pattern=[[-1, P]], compare_op=ALU.not_equal,
                                    fill=1.0, base=0, channel_multiplier=1).then_inc(s["ident_ready"], 1)
            for k in range(3):
                pool.dma_start(pos[k * NTOK:(k + 1) * NTOK, :], a["L0_tok_pos_emb"]).then_inc(s["pos_loaded"], 16)
            row(bproj[:, :], "L0_tok_b_proj")
            row(bv[:, :], "L0_attn_bv")
            row(bo[:, :], "L0_attn_bo")
            row(baseb[:, :], "L0_ffn_base_b")
            row(routb[:, :], "L0_ffn_router_b")
            with nc.allow_non_contiguous_dma("per-feature vectors, four bytes a partition"):
                for dst, n in ((bq, "L0_attn_bq"), (bk, "L0_attn_bk"), (mur, "L1_ffn_mu_r"), (muk, "L1_ffn_mu_k")):
                    pool.dma_start(dst[:, :], a[n].rearrange("(t p) -> p t", p=P)).then_inc(s["vecs_loaded"], 16)
            c = [1]

            def link(ins):
                ins.then_inc(s["const_step"], 1)
                c[0] += 1
                pool.wait_ge(s["const_step"], c[0])

            nc.gpsimd.memset(mhalf[:, :], -0.5)
            nc.gpsimd.memset(mask01[:, :], 1.0)
            nc.gpsimd.memset(maskadd[:, :], 0.0)
            nc.gpsimd.memset(headmask[:, :], 1.0)
            link(nc.gpsimd.memset(blockones[:, :], 1.0))
            m01 = mask01[:, :].rearrange("p (b t) -> p b t", b=3)
            mad = maskadd[:, :].rearrange("p (b t) -> p b t", b=3)
            bl = blockones[:, :].rearrange("p (h d) -> p h d", h=HPT)
            hd = headmask[:, :]
            nc.gpsimd.affine_select(m01, m01, pattern=[[NTOK, 3], [1, NTOK]], compare_op=ALU.is_ge, fill=0.0,
                                    base=0, channel_multiplier=-1)
            nc.gpsimd.affine_select(mad, mad, pattern=[[-NTOK, 3], [-1, NTOK]], compare_op=ALU.is_ge, fill=NEG,
                                    base=0, channel_multiplier=1)
            nc.gpsimd.affine_select(hd, hd, pattern=[[-DH, HPT]], compare_op=ALU.is_ge, fill=0.0,
                                    base=0, channel_multiplier=1)
            link(nc.gpsimd.affine_select(bl, bl, pattern=[[-DH, HPT], [0, DH]], compare_op=ALU.is_ge, fill=0.0,
                                         base=0, channel_multiplier=1))
            nc.gpsimd.affine_select(m01, m01, pattern=[[-NTOK, 3], [0, NTOK]], compare_op=ALU.is_ge, fill=0.0,
                                    base=0, channel_multiplier=1)
            nc.gpsimd.affine_select(mad, mad, pattern=[[NTOK, 3], [0, NTOK]], compare_op=ALU.is_ge, fill=NEG,
                                    base=NTOK - 1, channel_multiplier=-1)
            nc.gpsimd.affine_select(hd, hd, pattern=[[DH, HPT]], compare_op=ALU.is_ge, fill=0.0,
                                    base=DH - 1, channel_multiplier=-1)
            nc.gpsimd.affine_select(bl, bl, pattern=[[DH, HPT], [0, DH]], compare_op=ALU.is_ge, fill=0.0,
                                    base=DH - 1, channel_multiplier=-1).then_inc(s["masks_ready"], 1)
            pool.wait_ge(s["pos_loaded"], 48)
            pool.wait_ge(s["rows_loaded"], 16 * 5)
            nc.gpsimd.tensor_tensor(pos[:, :], pos[:, :], bproj[:, :], ALU.add).then_inc(s["pos_ready"], 1)

            def rstd(n):
                def step(i):
                    for u in range(U):
                        t = T[u]
                        pool.wait_ge(ln[n].eps_added, U * i + u + 1)
                        nc.gpsimd.tensor_tensor(ln[n].rs[0:t, u:u + 1], ln[n].ve[0:t, u:u + 1], mhalf[0:t, :],
                                                ALU.pow).then_inc(ln[n].rstd_done, 1)
                return step

            def f_ln(i):
                rstd(0)(i)
                for u in range(U):
                    nc.gpsimd.tensor_tensor(hbo[0:T[u], u, :], hF[0:T[u], u, :], bo[0:T[u], :],
                                            ALU.add).then_inc(s["hbo_ready"], 1)

            def b_ln1(i):
                rstd(1)(i)
                for u in range(U):
                    nc.gpsimd.tensor_tensor(hbb[0:T[u], u, :], hB[0:T[u], u, :], baseb[0:T[u], :],
                                            ALU.add).then_inc(s["hbb_ready"], 1)

            def b_ln3(i):
                rstd(3)(i)
                for u in range(U):
                    n = IMGS[u]
                    pool.wait_ge(ln[3].xnT_ready, 2 * U * i + 2 * u + 2)
                    for k in range(KT):
                        xd_u = xd[:, u, k, 0:T[u]].rearrange("p (b t) -> p b t", b=n)
                        ins = nc.gpsimd.tensor_tensor(xd_u, xs[:, u, k, 0:n, 1:NTOK + 1], xs[:, u, k, 0:n, 0:NTOK],
                                                      ALU.subtract)
                    ins.then_inc(s["xd_ready"], 1)

            run(pool, {"F_ln": f_ln, "B_ln1": b_ln1, "B_ln2": rstd(2), "B_ln3": b_ln3})

        @block.tensor
        def _(pe):
            def w_g(_):
                qw, kw = wT["L1_attn_Qw"], wT["L1_attn_Kw"]
                pe.wait_ge(w_loaded["L1_attn_Qw"], 16)
                pe.wait_ge(w_loaded["L1_attn_Kw"], 16)
                for ft in range(KT):
                    for dt in range(KT):
                        ins = nc.tensor.matmul(bank[7][:, ft * E:(ft + 1) * E], qw[:, dt, ft * P:(ft + 1) * P],
                                               kw[:, dt, :], start=(dt == 0), stop=(dt == KT - 1))
                ins.then_inc(s["g_mm"], 1)
                for n in names[6:]:
                    pe.wait_ge(w_loaded[n], 16)
                pe.wait_ge(s["cat_loaded"], 16)
                pe.wait_ge(s["lora_loaded"], 16)
                pe.wait_ge(s["zeros_ready"], 1)
                pe.wait_ge(s["g_ready"], 1)

            def f_patch(i):
                if isinstance(i, int):
                    pe.wait_ge(s["wp_loaded"], 16)
                for u in range(U):
                    pe.wait_ge(x_loaded[u], 16 * i + 16)
                    for c in range(KC):
                        ins = nc.tensor.matmul(bank[TOK_BANK[u]][0:T[u], 0:E], xT[:, c, OFF[u]:OFF[u] + T[u]],
                                               wpT[:, c, :], start=(c == 0), stop=(c == KC - 1))
                    ins.then_inc(s["tok_mm"], 1)

            def turn_ln(n):
                def step(i):
                    for u in range(U):
                        pe.wait_ge(ln[n].xn_done, U * i + u + 1)
                        for k in range(KT):
                            ins = nc.tensor.transpose(tr(n, u)[:, k, :], ln[n].xn[0:T[u], u, k * P:(k + 1) * P],
                                                      ident[0:T[u], 0:T[u]])
                        ins.then_inc(ln[n].turned, 1)
                return step

            def f_qkv(i):
                xnT = ln[0].xnT

                def wide(w, ft, b, done):
                    for k in range(KT):
                        ins = nc.tensor.matmul(bank[b][:, 0:STOK], wT[w][:, k, ft * P:(ft + 1) * P], xnT[:, k, :],
                                               start=(k == 0), stop=(k == KT - 1))
                    ins.then_inc(s[done], 1)

                def values(u, b):
                    for k in range(KT):
                        ins = nc.tensor.matmul(bank[b][0:T[u], 0:E], xnT[:, k, OFF[u]:OFF[u] + T[u]],
                                               wT["L0_attn_Wv"][:, k, :], start=(k == 0), stop=(k == KT - 1))
                    ins.then_inc(s["v_mm"], 1)

                pe.wait_ge(ln[0].xnT_ready, U * i + U)
                if isinstance(i, int):
                    for n in names[:4]:
                        pe.wait_ge(w_loaded[n], 16)
                wide("L0_attn_Wk", 0, 3, "k_mm")
                wide("L0_attn_Wk", 1, 0, "k_mm")
                values(0, 4)
                values(1, 1)
                values(2, 2)
                pe.wait_ge(s["vpad_ready"], U * i + 1)
                wide("L0_attn_Wq", 0, 4, "q_mm")
                pe.wait_ge(s["vpad_ready"], U * i + 2)
                wide("L0_attn_Wq", 1, 1, "q_mm")

            SB = [2, 3, 0]

            def f_scores(i):
                def scores(u):
                    for ft in range(KT):
                        pe.wait_ge(s["qexp_ready"], KT * U * i + KT * u + ft + 1)
                        for half in range(2):
                            j = 4 * u + 2 * ft + half
                            if j == 0:
                                pe.wait_ge(s["vpad_ready"], U * i + 3)
                                pe.wait_ge(s["kT_ready"], KT * i + KT)
                            if j >= 3:
                                pe.wait_ge(s["s_masked"], 12 * i + j - 2)
                            nc.tensor.matmul(
                                bank[SB[j % 3]][0:T[u], 0:4 * T[u]].rearrange("p (h t) -> p h t", h=4),
                                kT[:, ft, OFF[u]:OFF[u] + T[u]],
                                qexp[:, ft, 4 * half:4 * half + 4, OFF[u]:OFF[u] + T[u]],
                                start=True, stop=True).then_inc(s["s_mm"], 1)

                def den(ft, b):
                    pe.wait_ge(s["qk_ready"], KT * i + ft + 1)
                    nc.tensor.matmul(bank[b][:, 0:STOK], blockones[:, :], qk[:, ft, :],
                                     start=True, stop=True).then_inc(s["den_mm"], 1)

                def numer(u):
                    pe.wait_ge(s["s_masked"], 12 * i + 4 * u + 4)
                    if u == 0:
                        pe.wait_ge(s["den_floor"], KT * i + KT)
                    else:
                        pe.wait_ge(s["attnT_ready"], U * i + u)
                    for ft in range(KT):
                        for r in range(4):
                            for e in range(2):
                                pair = 4 * ft + r
                                ins = nc.tensor.matmul(
                                    bank[1][32 * r:32 * r + 32, ft * T[u]:(ft + 1) * T[u]],
                                    vpad[0:T[u], u, pair, e, :, :].rearrange("p a d -> p (a d)"),
                                    S[0:T[u], u, 2 * pair + e, 0:T[u]], start=(e == 0), stop=(e == 1),
                                    tile_position=(0, 32 * r))
                    ins.then_inc(s["av_mm"], 1)

                scores(0)
                den(0, 4)
                scores(1)
                den(1, 1)
                numer(0)
                scores(2)
                numer(1)
                numer(2)

            def f_wo(i):
                for u in range(U):
                    pe.wait_ge(s["attnT_ready"], U * i + u + 1)
                    if u >= 1:
                        pe.wait_ge(s["h1_ready"], U * i + u)
                    for k in range(KT):
                        ins = nc.tensor.matmul(bank[4][0:T[u], 0:E], attnT[:, u, k, 0:T[u]],
                                               wT["L0_attn_Wo"][:, k, :], start=(k == 0), stop=(k == KT - 1))
                    ins.then_inc(s["wo_mm"], 1)

            def b_ffn(i):
                for u in range(U):
                    pe.wait_ge(ln[1].xnT_ready, U * i + u + 1)
                    for k in range(KT):
                        ins = nc.tensor.matmul(bank[FB + u][0:T[u], 0:NCAT], ln[1].xnT[:, k, OFF[u]:OFF[u] + T[u]],
                                               wcat[:, k, :], start=(k == 0), stop=(k == KT - 1))
                    ins.then_inc(s["ffn_mm"], 1)

            def b_lora(i):
                for u in range(U):
                    pe.wait_ge(s["z_ready"], U * i + u + 1)
                    pe.wait_ge(s["h2a_ready"], U * i + u + 1)
                    nc.tensor.transpose(bank[FB + u][:, 0:T[u]], z[0:T[u], u, :],
                                        ident[0:T[u], 0:T[u]]).then_inc(s["z_turned"], 1)
                for u in range(U):
                    pe.wait_ge(s["zT_ready"], U * i + u + 1)
                    nc.tensor.matmul(bank[FB + u][0:T[u], 0:E], zT[:, u, 0:T[u]], loraB[:, :],
                                     start=True, stop=True).then_inc(s["lora_mm"], 1)

            def b_atv(i):
                for u in range(U):
                    pe.wait_ge(ln[2].xnT_ready, U * i + u + 1)
                    for ft in range(KT):
                        for k in range(KT):
                            nc.tensor.matmul(bank[FB + u][:, ft * T[u]:(ft + 1) * T[u]],
                                             G[:, k, ft * P:(ft + 1) * P], ln[2].xnT[:, k, OFF[u]:OFF[u] + T[u]],
                                             start=(k == 0), stop=(k == KT - 1))
                    for k in range(KT):
                        ins = nc.tensor.matmul(bank[FB + u][0:T[u], E:2 * E], ln[2].xnT[:, k, OFF[u]:OFF[u] + T[u]],
                                               wT["L1_attn_Vw"][:, k, :], start=(k == 0), stop=(k == KT - 1))
                    ins.then_inc(s["atv_mm"], 1)

            def b_scores(i):
                for u in range(U):
                    pe.wait_ge(s["at_ready"], U * i + u + 1)
                    pe.wait_ge(s["v1_ready"], U * i + u + 1)
                    for k in range(KT):
                        ins = nc.tensor.matmul(bank[FB + u][0:T[u], 0:T[u]], at[:, u, k, 0:T[u]],
                                               ln[2].xnT[:, k, OFF[u]:OFF[u] + T[u]],
                                               start=(k == 0), stop=(k == KT - 1))
                    ins.then_inc(s["sc_mm"], 1)

            def b_pv(i):
                for u in range(U):
                    pe.wait_ge(s["prob_ready"], U * i + u + 1)
                    nc.tensor.transpose(bank[FB + u][0:T[u], 0:T[u]], prob[0:T[u], u, 0:T[u]],
                                        ident[0:T[u], 0:T[u]]).then_inc(s["prob_turned"], 1)
                for u in range(U):
                    pe.wait_ge(s["probT_ready"], U * i + u + 1)
                    nc.tensor.matmul(bank[FB + u][0:T[u], 0:E], probT[0:T[u], u, 0:T[u]], v1[0:T[u], u, :],
                                     start=True, stop=True).then_inc(s["pv_mm"], 1)

            def b_ffn1(i):
                for u in range(U):
                    pe.wait_ge(s["xr_ready"], U * i + u + 1)
                    for k in range(KT):
                        nc.tensor.matmul(bank[FB + u][0:T[u], 0:E], xr[:, u, k, 0:T[u]],
                                         wT["L1_ffn_W_r"][:, k, :], start=(k == 0), stop=(k == KT - 1))
                    pe.wait_ge(s["xk_ready"], U * i + u + 1)
                    for ft in range(KT):
                        for k in range(KT):
                            ins = nc.tensor.matmul(bank[FB + u][:, E + ft * T[u]:E + (ft + 1) * T[u]],
                                                   wT["L1_ffn_W_k"][:, k, ft * P:(ft + 1) * P],
                                                   xk[:, u, k, 0:T[u]], start=(k == 0), stop=(k == KT - 1))
                    ins.then_inc(s["rk_mm"], 1)

            def b_out(i):
                for u in range(U):
                    pe.wait_ge(s["kact_ready"], U * i + u + 1)
                    pe.wait_ge(s["rt_ready"], U * i + u + 1)
                    for k in range(KT):
                        ins = nc.tensor.matmul(bank[FB + u][0:T[u], 0:E], kact[:, u, k, 0:T[u]],
                                               wT["L1_ffn_W_v"][:, k, :], start=(k == 0), stop=(k == KT - 1))
                    ins.then_inc(s["kv_mm"], 1)

            pe.wait_ge(s["ident_ready"], 1)
            run(pe, {"F_patch": f_patch, "F_ln": turn_ln(0), "W_G": w_g, "F_qkv": f_qkv,
                     "F_scores": f_scores, "F_wo": f_wo, "B_ln1": turn_ln(1), "B_ffn": b_ffn, "B_lora": b_lora,
                     "B_ln2": turn_ln(2), "B_atv": b_atv, "B_scores": b_scores, "B_pv": b_pv,
                     "B_ln3": turn_ln(3), "B_ffn1": b_ffn1, "B_out": b_out})

        @block.scalar
        def _(act):
            def copy(dst, src):
                return nc.scalar.activation(dst, src, ACT.Copy)

            def w_g(_):
                act.wait_ge(s["g_mm"], 1)
                copy(G[:, :, :], bank[7][:, :].rearrange("p (k e) -> p k e", k=KT)).then_inc(s["g_ready"], 1)

            def take_ln(n):
                def step(i):
                    for u in range(U):
                        act.wait_ge(ln[n].turned, U * i + u + 1)
                        if n == 3:
                            for k in range(KT):
                                copy(xs[:, u, k, 0:IMGS[u], 1:NTOK + 1],
                                     tr(n, u)[:, k, :].rearrange("p (b t) -> p b t", b=IMGS[u])
                                     ).then_inc(ln[n].xnT_ready, 1)
                        else:
                            copy(ln[n].xnT[:, :, OFF[u]:OFF[u] + T[u]], tr(n, u)).then_inc(ln[n].xnT_ready, 1)
                return step

            def f_qkv(i):
                for name, src in (("k", kmin), ("q", qmin)):
                    for ft in range(KT):
                        act.wait_ge(s[f"{name}_min"], KT * i + ft + 1)
                        nc.scalar.activation(src[:, ft, :], src[:, ft, :], ACT.Exp).then_inc(s[f"{name}_exp"], 1)

            def b_ffn(i):
                for u in range(U):
                    t = T[u]
                    act.wait_ge(s["lsub_ready"], U * i + u + 1)
                    nc.scalar.activation(lexp[0:t, u, :], lsub[0:t, u, :], ACT.Exp,
                                         accum_out=lsum[0:t, u:u + 1]).then_inc(s["lexp_ready"], 1)

            def b_lora(i):
                for u in range(U):
                    act.wait_ge(s["z_turned"], U * i + u + 1)
                    copy(zT[:, u, 0:T[u]], bank[FB + u][:, 0:T[u]]).then_inc(s["zT_ready"], 1)

            def b_atv(i):
                for u in range(U):
                    t = T[u]
                    act.wait_ge(s["atv_mm"], U * i + u + 1)
                    copy(at[:, u, :, 0:t], bank[FB + u][:, 0:KT * t].rearrange("p (k t) -> p k t", k=KT)
                         ).then_inc(s["at_ready"], 1)
                    copy(v1[0:t, u, :], bank[FB + u][0:t, E:2 * E]).then_inc(s["v1_ready"], 1)

            def b_scores(i):
                for u in range(U):
                    t = T[u]
                    act.wait_ge(s["nmax_ready"], U * i + u + 1)
                    nc.scalar.activation(prob[0:t, u, 0:t], sm[0:t, u, 0:t], ACT.Exp, bias=nmax[0:t, u:u + 1],
                                         scale=float(E) ** -0.5, accum_out=psm[0:t, u:u + 1]
                                         ).then_inc(s["prob_ready"], 1)

            def b_pv(i):
                for u in range(U):
                    act.wait_ge(s["prob_turned"], U * i + u + 1)
                    copy(probT[0:T[u], u, 0:T[u]], bank[FB + u][0:T[u], 0:T[u]]).then_inc(s["probT_ready"], 1)

            def b_ffn1(i):
                for u in range(U):
                    t = T[u]
                    act.wait_ge(s["rk_mm"], U * i + u + 1)
                    nc.scalar.activation(kact[:, u, :, 0:t],
                                         bank[FB + u][:, E:E + KT * t].rearrange("p (k t) -> p k t", k=KT),
                                         ACT.Relu).then_inc(s["krelu_ready"], 1)
                    nc.scalar.activation(rt[0:t, u, :], bank[FB + u][0:t, 0:E], ACT.Tanh, scale=0.5
                                         ).then_inc(s["rt_ready"], 1)

            run(act, {"F_ln": take_ln(0), "W_G": w_g, "F_qkv": f_qkv,
                      "B_ln1": take_ln(1), "B_ffn": b_ffn, "B_lora": b_lora, "B_ln2": take_ln(2),
                      "B_atv": b_atv, "B_scores": b_scores, "B_pv": b_pv, "B_ln3": take_ln(3),
                      "B_ffn1": b_ffn1})

        @block.vector
        def _(dve):
            nc.vector.memset(vpad[:, :, :, :, :, :], 0.0)
            nc.vector.memset(z[:, :, :], 0.0)
            for u in range(U):
                nc.vector.memset(o_sb[:, u, 0:1], 0.0).then_inc(out_stored[u], 1)
            nc.vector.memset(xs[:, :, :, :, 0:1], 0.0)
            nc.vector.memset(restart[:, :], 1.0)
            nc.vector.memset(loraB[NE * R:P, :], 0.0).then_inc(s["zeros_ready"], 1)
            dve.wait_ge(s["zeros_ready"], 1)
            rs_v = restart[:, :].rearrange("p (b t) -> p b t", b=STEP_IMGS)
            nc.vector.memset(rs_v[:, :, 0:1], 0.0).then_inc(s["zeros_ready"], 1)
            dve.wait_ge(s["vecs_loaded"], 64)
            nc.vector.tensor_scalar(bk1[:, :], bk[:, :], 1.0, None, ALU.add)
            nc.vector.tensor_scalar(bq1[:, :], bq[:, :], 1.0, None, ALU.add).then_inc(s["bias1_ready"], 1)
            dve.wait_ge(s["bias1_ready"], 1)
            dve.wait_ge(s["zeros_ready"], 2)
            dve.wait_ge(s["masks_ready"], 1)
            dve.wait_ge(s["pos_ready"], 1)

            def ln_stats(n, i, u, h, h_ready):
                L, t, c = ln[n], T[u], U * i + u + 1
                dve.wait_ge(h_ready, c)
                nc.vector.bn_stats(L.st[0:t, u, :], h[0:t, u, :]).then_inc(L.stats_done, 1)
                dve.wait_ge(s["pos_ready"], 1)
                dve.wait_ge(L.stats_done, c)
                nc.vector.bn_aggr(L.mv[0:t, u, :], L.st[0:t, u, :]).then_inc(L.var_done, 1)
                dve.wait_ge(L.var_done, c)
                nc.vector.tensor_scalar(L.ve[0:t, u:u + 1], L.mv[0:t, u, 1:2], LN_EPS, None,
                                        ALU.add).then_inc(L.eps_added, 1)

            def ln_apply(n, i, u, h):
                L, t, c = ln[n], T[u], U * i + u + 1
                dve.wait_ge(L.rstd_done, c)
                nc.vector.tensor_scalar(L.xn[0:t, u, :], h[0:t, u, :], L.mv[0:t, u, 0:1], L.rs[0:t, u:u + 1],
                                        ALU.subtract, ALU.mult).then_inc(L.xn_done, 1)

            def norm(n, h, name):
                def step(i):
                    ln_stats(n, i, 0, h, s[name])
                    ln_stats(n, i, 1, h, s[name])
                    ln_apply(n, i, 0, h)
                    ln_stats(n, i, 2, h, s[name])
                    ln_apply(n, i, 1, h)
                    ln_apply(n, i, 2, h)
                return step

            def f_patch(i):
                def take_h(u):
                    t = T[u]
                    dve.wait_ge(s["tok_mm"], U * i + u + 1)
                    nc.vector.tensor_tensor(hF[0:t, u, :], bank[TOK_BANK[u]][0:t, 0:E], pos[0:t, :],
                                            ALU.add).then_inc(s["hF_ready"], 1)

                for u in range(U):
                    take_h(u)

            def f_qkv(i):
                def floor(name, ft, b, bias, dst):
                    dve.wait_ge(s[f"{name}_mm"], KT * i + ft + 1)
                    nc.vector.tensor_scalar(dst[:, ft, :], bank[b][:, 0:STOK], bias[:, ft:ft + 1], 0.0,
                                            ALU.add, ALU.min).then_inc(s[f"{name}_min"], 1)

                def feature(name, ft, b, bias1, src, dst):
                    dve.wait_ge(s[f"{name}_exp"], KT * i + ft + 1)
                    nc.vector.scalar_tensor_tensor(out=dst[:, ft, :], in0=bank[b][:, 0:STOK],
                                                   scalar=bias1[:, ft:ft + 1], in1=src[:, ft, :],
                                                   op0=ALU.add, op1=ALU.max).then_inc(s[f"{name}T_ready"], 1)

                def values(u, b):
                    t = T[u]
                    dve.wait_ge(s["v_mm"], U * i + u + 1)
                    for e in range(2):
                        ins = nc.vector.tensor_tensor(
                            vpad[0:t, u, :, e, e, :],
                            bank[b][0:t, 0:E].rearrange("p (j e d) -> p j e d", e=2, d=DH)[:, :, e, :],
                            bv[0:t, :].rearrange("p (j e d) -> p j e d", e=2, d=DH)[:, :, e, :], ALU.add)
                    ins.then_inc(s["vpad_ready"], 1)

                floor("k", 0, 3, bk, kmin)
                floor("k", 1, 0, bk, kmin)
                values(0, 4)
                feature("k", 0, 3, bk1, kmin, kT)
                values(1, 1)
                feature("k", 1, 0, bk1, kmin, kT)
                values(2, 2)
                floor("q", 0, 4, bq, qmin)
                floor("q", 1, 1, bq, qmin)
                for ft in range(KT):
                    dve.wait_ge(s["kT_ready"], KT * i + ft + 1)
                    nc.vector.tensor_tensor_scan(kcum[:, ft, :], restart[:, :], kT[:, ft, :], 0.0,
                                                 ALU.mult, ALU.add).then_inc(s["kcum_ready"], 1)
                feature("q", 0, 4, bq1, qmin, qT)
                feature("q", 1, 1, bq1, qmin, qT)

            def f_scores(i):
                def spread(u, ft):
                    o, t = OFF[u], T[u]
                    dve.wait_ge(s["qT_ready"], KT * i + ft + 1)
                    nc.vector.tensor_tensor(
                        qexp[:, ft, :, o:o + t], qT[:, ft:ft + 1, o:o + t].to_broadcast([P, HPT, t]),
                        headmask[:, :].rearrange("p (h o) -> p h o", o=1).to_broadcast([P, HPT, t]),
                        ALU.mult).then_inc(s["qexp_ready"], 1)

                def mask(u, j4):
                    j, t = 4 * u + j4, T[u]
                    dve.wait_ge(s["s_mm"], 12 * i + j + 1)
                    nc.vector.tensor_tensor(
                        S[0:t, u, 4 * j4:4 * j4 + 4, 0:t],
                        bank[[2, 3, 0][j % 3]][0:t, 0:4 * t].rearrange("p (h t) -> p h t", h=4),
                        mask01[0:t, 0:t].rearrange("p (o t) -> p o t", o=1).to_broadcast([t, 4, t]),
                        ALU.mult).then_inc(s["s_masked"], 1)

                def q_times_k(ft):
                    dve.wait_ge(s["kcum_ready"], KT * i + ft + 1)
                    nc.vector.tensor_tensor(qk[:, ft, :], qT[:, ft, :], kcum[:, ft, :],
                                            ALU.mult).then_inc(s["qk_ready"], 1)

                def den(ft, b):
                    dve.wait_ge(s["den_mm"], KT * i + ft + 1)
                    nc.vector.tensor_scalar(rden[:, ft, :], bank[b][:, 0:STOK], DEN_EPS, None,
                                            ALU.max).then_inc(s["den_floor"], 1)
                    dve.wait_ge(s["den_floor"], KT * i + ft + 1)
                    nc.vector.reciprocal(rden[:, ft, :], rden[:, ft, :]).then_inc(s["rden_ready"], 1)

                def divide(u):
                    o, t = OFF[u], T[u]
                    dve.wait_ge(s["rden_ready"], KT * i + KT)
                    dve.wait_ge(s["av_mm"], U * i + u + 1)
                    nc.vector.tensor_tensor(attnT[:, u, :, 0:t],
                                            bank[1][:, 0:KT * t].rearrange("p (k t) -> p k t", k=KT),
                                            rden[:, :, o:o + t], ALU.mult).then_inc(s["attnT_ready"], 1)

                spread(0, 0)
                spread(0, 1)
                q_times_k(0)
                q_times_k(1)
                mask(0, 0)
                mask(0, 1)
                spread(1, 0)
                mask(0, 2)
                mask(0, 3)
                spread(1, 1)
                den(0, 4)
                mask(1, 0)
                mask(1, 1)
                mask(1, 2)
                mask(1, 3)
                spread(2, 0)
                spread(2, 1)
                den(1, 1)
                for j4 in range(4):
                    mask(2, j4)
                for u in range(U):
                    divide(u)

            def f_wo(i):
                for u in range(U):
                    t = T[u]
                    dve.wait_ge(s["wo_mm"], U * i + u + 1)
                    dve.wait_ge(s["hbo_ready"], U * i + u + 1)
                    nc.vector.tensor_tensor(hB[0:t, u, :], bank[4][0:t, 0:E], hbo[0:t, u, :],
                                            ALU.add).then_inc(s["h1_ready"], 1)

            def b_ffn(i):
                def first(u):
                    t, b, c = T[u], FB + u, U * i + u + 1
                    dve.wait_ge(s["ffn_mm"], c)
                    nc.vector.tensor_tensor(logit[0:t, u, :], bank[b][0:t, E:E + NE], routb[0:t, :],
                                            ALU.add).then_inc(s["logit_ready"], 1)
                    nc.vector.tensor_scalar(mid[0:t, u, :], bank[b][0:t, E + NE:NCAT], LORA_SCALING, None,
                                            ALU.mult).then_inc(s["mid_ready"], 1)
                    dve.wait_ge(s["logit_ready"], c)
                    nc.vector.tensor_reduce(lmax[0:t, u:u + 1], logit[0:t, u, :], AX, ALU.max
                                            ).then_inc(s["lmax_ready"], 1)
                    dve.wait_ge(s["lmax_ready"], c)
                    nc.vector.tensor_scalar(lsub[0:t, u, :], logit[0:t, u, :], lmax[0:t, u:u + 1], None,
                                            ALU.subtract).then_inc(s["lsub_ready"], 1)
                    dve.wait_ge(s["hbb_ready"], c)
                    nc.vector.tensor_tensor(hB[0:t, u, :], bank[b][0:t, 0:E], hbb[0:t, u, :],
                                            ALU.add).then_inc(s["h2a_ready"], 1)

                def second(u):
                    t, c = T[u], U * i + u + 1
                    dve.wait_ge(s["lexp_ready"], c)
                    nc.vector.reciprocal(lrec[0:t, u:u + 1], lsum[0:t, u:u + 1]).then_inc(s["lrec_ready"], 1)
                    dve.wait_ge(s["lrec_ready"], c)
                    nc.vector.tensor_scalar(gate[0:t, u, :], lexp[0:t, u, :], lrec[0:t, u:u + 1], None,
                                            ALU.mult).then_inc(s["gate_ready"], 1)
                    dve.wait_ge(s["gate_ready"], c)
                    dve.wait_ge(s["mid_ready"], c)
                    nc.vector.tensor_tensor(
                        z[0:t, u, 0:NE * R].rearrange("p (e r) -> p e r", e=NE),
                        gate[0:t, u, :].rearrange("p (e o) -> p e o", o=1).to_broadcast([t, NE, R]),
                        mid[0:t, u:u + 1, :].to_broadcast([t, NE, R]), ALU.mult).then_inc(s["z_ready"], 1)

                first(0)
                first(1)
                second(0)
                first(2)
                second(1)
                second(2)

            def b_lora(i):
                for u in range(U):
                    t, c = T[u], U * i + u + 1
                    dve.wait_ge(s["lora_mm"], c)
                    dve.wait_ge(s["h2a_ready"], c)
                    nc.vector.tensor_tensor(hB[0:t, u, :], bank[FB + u][0:t, 0:E], hB[0:t, u, :],
                                            ALU.add).then_inc(s["h2_ready"], 1)

            def b_scores(i):
                for u in range(U):
                    t, c = T[u], U * i + u + 1
                    dve.wait_ge(s["sc_mm"], c)
                    nc.vector.tensor_tensor(sm[0:t, u, 0:t], bank[FB + u][0:t, 0:t], maskadd[0:t, 0:t],
                                            ALU.add).then_inc(s["sm_ready"], 1)
                    dve.wait_ge(s["sm_ready"], c)
                    nc.vector.tensor_reduce(smax[0:t, u:u + 1], sm[0:t, u, 0:t], AX, ALU.max
                                            ).then_inc(s["smax_ready"], 1)
                    dve.wait_ge(s["smax_ready"], c)
                    nc.vector.tensor_scalar(nmax[0:t, u:u + 1], smax[0:t, u:u + 1], -float(E) ** -0.5, None,
                                            ALU.mult).then_inc(s["nmax_ready"], 1)

            def b_pv(i):
                for u in range(U):
                    t, c = T[u], U * i + u + 1
                    dve.wait_ge(s["prob_ready"], c)
                    nc.vector.reciprocal(prec[0:t, u:u + 1], psm[0:t, u:u + 1]).then_inc(s["prec_ready"], 1)
                for u in range(U):
                    t, c = T[u], U * i + u + 1
                    dve.wait_ge(s["prec_ready"], c)
                    dve.wait_ge(s["pv_mm"], c)
                    nc.vector.scalar_tensor_tensor(out=hB[0:t, u, :], in0=bank[FB + u][0:t, 0:E],
                                                   scalar=prec[0:t, u:u + 1], in1=hB[0:t, u, :],
                                                   op0=ALU.mult, op1=ALU.add).then_inc(s["h3_ready"], 1)

            def b_ffn1(i):
                def mix(u, name, dst, mu):
                    n = IMGS[u]
                    dve.wait_ge(s["xd_ready"], U * i + u + 1)
                    for k in range(KT):
                        ins = nc.vector.scalar_tensor_tensor(
                            out=dst[:, u, k, 0:T[u]].rearrange("p (b t) -> p b t", b=n),
                            in0=xd[:, u, k, 0:T[u]].rearrange("p (b t) -> p b t", b=n), scalar=mu[:, k:k + 1],
                            in1=xs[:, u, k, 0:n, 0:NTOK], op0=ALU.mult, op1=ALU.add)
                    ins.then_inc(s[name], 1)

                def square(u):
                    t = T[u]
                    dve.wait_ge(s["krelu_ready"], U * i + u + 1)
                    nc.vector.tensor_tensor(kact[:, u, :, 0:t], kact[:, u, :, 0:t], kact[:, u, :, 0:t],
                                            ALU.mult).then_inc(s["kact_ready"], 1)

                for u in range(U):
                    mix(u, "xr_ready", xr, mur)
                    mix(u, "xk_ready", xk, muk)
                for u in range(U):
                    square(u)

            def b_out(i):
                for u in range(U):
                    t, c = T[u], U * i + u + 1
                    dve.wait_ge(s["kv_mm"], c)
                    dve.wait_ge(s["rt_ready"], c)
                    nc.vector.scalar_tensor_tensor(out=rt[0:t, u, :], in0=rt[0:t, u, :], scalar=1.0,
                                                   in1=bank[FB + u][0:t, 0:E], op0=ALU.add, op1=ALU.mult
                                                   ).then_inc(s["rkv_ready"], 1)
                    dve.wait_ge(s["rkv_ready"], c)
                    dve.wait_ge(out_stored[u], 16 * i + 1)
                    nc.vector.scalar_tensor_tensor(out=o_sb[0:t, u, :], in0=rt[0:t, u, :], scalar=0.5,
                                                   in1=hB[0:t, u, :], op0=ALU.mult, op1=ALU.add
                                                   ).then_inc(s["out_ready"], 1)

            run(dve, {"F_patch": f_patch, "F_ln": norm(0, hF, "hF_ready"), "F_qkv": f_qkv, "F_scores": f_scores,
                      "F_wo": f_wo, "B_ln1": norm(1, hB, "h1_ready"), "B_ffn": b_ffn, "B_lora": b_lora,
                      "B_ln2": norm(2, hB, "h2_ready"), "B_scores": b_scores, "B_pv": b_pv,
                      "B_ln3": norm(3, hB, "h3_ready"), "B_ffn1": b_ffn1, "B_out": b_out})


def kernel(**inputs):
    import numpy as _np
    import concourse.bacc as _bacc
    from concourse import mybir as _mybir
    from concourse.bass_utils import run_bass_kernel_spmd as _run

    host = {n: _np.asarray(v) for n, v in inputs.items()}
    x = host["x"].reshape(B, GRID, PATCH, GRID, PATCH, C).transpose(0, 1, 3, 2, 4, 5)
    x = x.reshape(STEPS, STOK, KC, P).transpose(0, 3, 2, 1).reshape(STEPS * P, KC, STOK)
    laid = {"x": x}
    for n in ("L0_tok_W_proj", "L0_attn_Wk", "L0_attn_Wv", "L0_attn_Wq", "L0_attn_Wo", "L1_attn_Qw", "L1_attn_Kw",
              "L1_ffn_W_r", "L1_ffn_W_k", "L1_ffn_W_v"):
        laid[n] = host[n].T
    laid["L0_ffn_cat"] = _np.concatenate([host["L0_ffn_base_w"].T, host["L0_ffn_router_w"].T,
                                          host["L0_ffn_lora_A"]], axis=1)
    laid["L0_ffn_lora_B"] = host["L0_ffn_lora_B"].reshape(NE * R, E)
    for n in ("L1_attn_Vw", "L0_tok_b_proj", "L0_tok_pos_emb", "L0_attn_bq", "L0_attn_bk", "L0_attn_bv", "L0_attn_bo",
              "L0_ffn_base_b", "L0_ffn_router_b", "L1_ffn_mu_r", "L1_ffn_mu_k"):
        laid[n] = host[n]

    nc = _bacc.Bacc("TRN2", target_bir_lowering=False, num_devices=1)
    arrays, args = {}, {}
    for name, v in laid.items():
        v = _np.ascontiguousarray(v)
        arrays[f"in_{name}_dram"] = v
        args[name] = nc.dram_tensor(f"in_{name}_dram", v.shape, _mybir.dt.from_np(v.dtype), kind="ExternalInput").ap()
    args["out"] = nc.dram_tensor("out_0_dram", (B, NTOK, E), F32, kind="ExternalOutput").ap()
    vit_tower_kernel(nc, args)
    r = _run(nc, [arrays], core_ids=[0])
    return r.results[0]["out_0_dram"]
```

```python
from contextlib import ExitStack

import concourse.bass as bass
from concourse import mybir

F32 = mybir.dt.float32
BF16 = mybir.dt.bfloat16
F32R = mybir.dt.float32r
ALU = mybir.AluOpType
ACT = mybir.ActivationFunctionType
AX = mybir.AxisListType.X

P = 128
B, HW, C = 32, 96, 3
PATCH = 16
GRID = HW // PATCH
NTOK = GRID * GRID
PD = PATCH * PATCH * C
KC = PD // P
E = 256
KT = E // P
NH, DH = 16, 16
HPT = P // DH
NE, R = 8, 8
LORA_SCALING = 16.0 / R
LN_EPS = 1e-5
DEN_EPS = 1e-6
STEP_IMGS = 8
STEPS = B // STEP_IMGS
STOK = STEP_IMGS * NTOK
IMGS = [3, 3, 2]
U = len(IMGS)
T = [n * NTOK for n in IMGS]
OFF = [0, T[0], T[0] + T[1]]
TMAX = max(T)
NEG = -1e30
FB = 5


PE_BODY = """
    B_tr1.0 B_tr1.1 B_tr1.2 B_ffn0 B_ffn1 B_ffn2 B_z0 B_z1 F_tok0 F_tok1 B_lora0 B_lora1 F_tok2 B_z2
    B_tr2.0 B_lora2 B_atv0 F_tr0.0 F_tr0.1 F_tr0.2 B_tr2.1 B_sc0 F_k0 F_k1 F_q0 B_atv1 B_pt0 B_tr2.2
    F_q1 B_pv0 F_v0 B_sc1 B_atv2 F_v1 B_pt1 B_tr3.0 B_sc2 B_pv1 F_v2 F_sc0 F_sc1 B_pt2 F_den0 B_pv2
    F_den1 F_sc2 B_rk0 B_tr3.1 F_sc3 F_av0 B_out0 F_sc4 B_tr3.2 B_rk1 F_wo0 F_sc5 F_av1 B_rk2 B_out1
    F_wo1 F_av2 B_out2 F_wo2
"""
ACT_BODY = """
    B_ct1.0 B_ct1.1 B_ct1.2 F_x0 F_x1 B_ffn0 B_ffn1 B_ffn2 F_x2 B_z0 B_z1 B_ap2.0 B_z2 F_ap0.0
    B_ct2.0 B_ap2.1 F_ap0.1 F_ap0.2 B_atv0 F_ct0.0 F_ct0.1 F_ct0.2 F_k0 B_ct2.1 F_k1 F_q0 B_ap2.2
    B_sc0 B_pt0 B_atv1 B_ct2.2 F_q1 B_sc1 B_ap3.0 B_atv2 B_pt1 B_ct3.0 B_sc2 B_pt2 B_ap3.1 B_rk0
    B_ct3.1 B_ap3.2 B_ct3.2 B_rk1 B_rk2 F_ap1.0 F_ap1.1 F_ap1.2
"""
DVE_BODY = """
    B_ffn0 B_lmax0 B_lsub0 B_h2a0 B_lrec0 B_ffn1 B_lmax1 B_gate0 B_z0 B_lsub1 B_h2a1 B_lrec1 B_gate1
    B_z1 B_ffn2 B_lmax2 B_lsub2 B_h2a2 B_lrec2 B_gate2 B_z2 F_tok0 F_st0.0 F_mv0.0 F_ve0.0 B_lora0
    B_st2.0 B_mv2.0 B_ve2.0 B_lora1 B_st2.1 B_mv2.1 F_tok1 F_st0.1 B_ve2.1 F_mv0.1 F_ve0.1 F_tok2
    F_st0.2 F_mv0.2 F_ve0.2 F_lo0 F_lo1 F_lo2 B_lora2 B_sc0 B_st2.2 B_mv2.2 F_k0 B_smax0 B_ve2.2
    F_cum0 F_k1 B_nmax0 F_cum1 F_q0 F_spr0 B_prec0 B_pv0 B_st3.0 B_mv3.0 B_sc1 B_ve3.0 F_v0 B_smax1
    B_nmax1 F_qk0 F_q1 F_spr1 F_v1 B_sc2 B_prec1 B_smax2 B_pv1 B_nmax2 B_st3.1 F_v2 F_qk1 F_sc0
    B_mv3.1 B_ve3.1 B_prec2 B_xr0 B_xk0 F_sc1 F_fl0 B_pv2 B_st3.2 F_fl1 F_sc2 B_mv3.2 F_rc0 B_rk0
    B_ve3.2 F_sc3 B_xr1 B_xk1 F_rc1 F_av0 B_rkv0 B_out0 B_xr2 B_xk2 F_sc4 F_sc5 F_wo0 F_st1.0
    F_mv1.0 F_ve1.0 B_rk1 F_av1 B_rk2 B_rkv1 B_out1 F_wo1 F_st1.1 F_mv1.1 F_ve1.1 F_av2 B_rkv2
    B_out2 F_wo2 F_st1.2 F_mv1.2 F_ve1.2
"""
POOL_BODY = """
    F_x0 F_x1 F_x2 B_rs2.0 F_rs0.0 B_rs2.1 F_rs0.1 F_rs0.2 F_hbo0 B_rs2.2 B_rs3.0 F_hbo1 F_hbo2
    F_spread2 B_xd0 B_rs3.1 F_spread3 F_spread4 B_xd1 B_rs3.2 B_xd2 F_spread5 F_rs1.0 F_hbb0 F_rs1.1
    F_hbb1 F_rs1.2 F_hbb2
"""


def vit_tower_kernel(nc, a):
    out = a["out"].rearrange("b n e -> (b n) e")

    ctx = ExitStack()
    with ctx:
        def sb(name, shape, dt=F32):
            return ctx.enter_context(nc.sbuf_tensor(name, shape, dt))

        def sem(name):
            return ctx.enter_context(nc.semaphore(name))

        bank = [ctx.enter_context(nc.psum_tensor(f"bank{k}", [P, 512], F32)) for k in range(8)]

        names = ["L0_attn_Wk", "L0_attn_Wv", "L0_attn_Wq", "L0_attn_Wo",
                 "L1_attn_Qw", "L1_attn_Kw", "L1_attn_Vw", "L1_ffn_W_r", "L1_ffn_W_k", "L1_ffn_W_v"]
        wp_hi, wp_lo = sb("wp_hi", [P, KC, E], F32R), sb("wp_lo", [P, KC, E], F32R)
        SPLIT = names[:3]
        w_hi = {n: sb(n + "_hi", [P, KT, E], F32R) for n in SPLIT}
        w_lo = {n: sb(n + "_lo", [P, KT, E], F32R) for n in SPLIT}
        wT = {n: sb(n + "_T", [P, KT, E]) for n in names[3:]}
        NCAT = E + NE + R
        wcat = sb("wcat", [P, KT, NCAT])
        G = sb("G", [P, KT, E])
        loraB = sb("loraB", [P, E])

        ident = sb("ident", [P, P])
        pos = sb("pos", [TMAX, E])
        bproj = sb("bproj", [TMAX, E])
        bv = sb("bv", [TMAX, E])
        bo = sb("bo", [TMAX, E])
        baseb = sb("baseb", [TMAX, E])
        routb = sb("routb", [TMAX, NE])
        bq = sb("bq", [P, KT])
        bk = sb("bk", [P, KT])
        bq1 = sb("bq1", [P, KT])
        bk1 = sb("bk1", [P, KT])
        nbq = sb("nbq", [P, KT])
        nbk = sb("nbk", [P, KT])
        mur = sb("mur", [P, KT])
        muk = sb("muk", [P, KT])
        mask01 = sb("mask01", [TMAX, TMAX])
        maskadd = sb("maskadd", [TMAX, TMAX])
        headmask = sb("headmask", [P, HPT])
        blockones = sb("blockones", [P, P])
        restart = sb("restart", [P, STOK])
        mhalf = sb("mhalf", [TMAX, 1])

        xT = sb("xT", [P, KC, STOK])
        x_hi, x_lo = sb("x_hi", [P, KC, STOK], F32R), sb("x_lo", [P, KC, STOK], F32R)
        xn0_hi, xn0_lo = sb("xn0_hi", [P, KT, STOK], F32R), sb("xn0_lo", [P, KT, STOK], F32R)
        hF = sb("hF", [TMAX, U, E])
        hbo = sb("hbo", [TMAX, U, E])
        kT = sb("kT", [P, KT, STOK])
        qT = sb("qT", [P, KT, STOK])
        qexp = sb("qexp", [P, KT, HPT, STOK])
        vpad = sb("vpad", [TMAX, U, NH // 2, 2, 2, DH])
        kcum = sb("kcum", [P, KT, STOK])
        kmin = kcum
        qk = sb("qk", [P, KT, STOK])
        qmin = qk
        rden = sb("rden", [P, KT, STOK])
        S = sb("S", [P, U, NH, TMAX])
        staged = S[:, :, :, :].rearrange("p u h t -> p (u h t)")
        wp_raw = staged[:, 0:KC * E].rearrange("p (c e) -> p c e", c=KC)
        w_raw = {n: staged[:, (KC + KT * j) * E:(KC + KT * (j + 1)) * E].rearrange("p (k e) -> p k e", k=KT)
                 for j, n in enumerate(SPLIT)}
        attnT = sb("attnT", [P, U, KT, TMAX])
        hB = sb("hB", [TMAX, U, E])
        hbb = sb("hbb", [TMAX, U, E])
        logit = sb("logit", [TMAX, U, NE])
        lmax = sb("lmax", [TMAX, U])
        lsub = sb("lsub", [TMAX, U, NE])
        lexp = sb("lexp", [TMAX, U, NE])
        lsum = sb("lsum", [TMAX, U])
        lrec = sb("lrec", [TMAX, U])
        gate = sb("gate", [TMAX, U, NE], BF16)
        mid = sb("mid", [TMAX, U, R])
        z = sb("z", [TMAX, U, P])
        zT = sb("zT", [P, U, TMAX])
        at = sb("at", [P, U, KT, TMAX])
        v1 = sb("v1", [TMAX, U, E])
        sm = sb("sm", [TMAX, U, TMAX])
        smax = sb("smax", [TMAX, U])
        nmax = sb("nmax", [TMAX, U])
        prob = sb("prob", [TMAX, U, TMAX])
        psm = sb("psm", [TMAX, U])
        prec = sb("prec", [TMAX, U])
        probT = sb("probT", [TMAX, U, TMAX])
        xs = sb("xs", [P, U, KT, 3, NTOK + 1])
        xd = sb("xd", [P, U, KT, TMAX])
        xr = sb("xr", [P, U, KT, TMAX])
        xk = sb("xk", [P, U, KT, TMAX])
        rt = sb("rt", [TMAX, U, E])
        kact = sb("kact", [P, U, KT, TMAX])
        o_sb = sb("o_sb", [TMAX, U, E])

        xn_back = sb("xn_back", [TMAX, U, E])
        xnT_back = sb("xnT_back", [P, KT, STOK])

        class LN:
            def __init__(self, n):
                self.st = sb(f"ln{n}_st", [TMAX, U, 6])
                self.mv = sb(f"ln{n}_mv", [TMAX, U, 2])
                self.ve = sb(f"ln{n}_ve", [TMAX, U])
                self.nm = sb(f"ln{n}_nm", [TMAX, U])
                self.nb = sb(f"ln{n}_nb", [TMAX, U])
                self.rs = sb(f"ln{n}_rs", [TMAX, U])
                self.xn = xn_back if n else sb("xn_front", [TMAX, U, E])
                self.xnT = xnT_back if n else None
                self.stats_done = sem(f"ln{n}_stats_done")
                self.var_done = sem(f"ln{n}_var_done")
                self.pre_done = sem(f"ln{n}_pre_done")
                self.rstd_done = sem(f"ln{n}_rstd_done")
                self.xn_done = sem(f"ln{n}_xn_done")
                self.turned = sem(f"ln{n}_turned")
                self.xnT_ready = sem(f"ln{n}_xnT_ready")

        ln = [LN(n) for n in range(4)]

        s = {n: sem(n) for n in [
            "wp_loaded", "wp_hi_ready", "wp_lo_ready", "w_hi_ready", "w_lo_ready", "cat_loaded", "lora_loaded", "pos_loaded", "rows_loaded", "vecs_loaded",
            "const_step", "ident_ready", "masks_ready", "zeros_ready", "pos_ready", "bias1_ready",
            "g_mm", "g_ready",
            "x_hi_ready", "x_lo_ready", "xn0_lo_ready", "tok_mm", "hF_ready", "k_mm", "k_min", "k_exp", "kT_ready",
            "q_mm", "q_min", "q_exp", "qT_ready", "v_mm", "vpad_ready", "qexp_ready", "qexp_pool", "kcum_ready",
            "qk_ready", "den_mm", "den_floor", "rden_ready", "s_mm", "s_masked", "av_mm", "attnT_ready",
            "wo_mm", "hbo_ready", "h1_ready",
            "ffn_mm", "logit_ready", "lmax_ready", "lsub_ready", "lexp_ready", "lrec_ready", "gate_ready",
            "mid_ready", "z_ready", "hbb_ready", "h2a_ready", "z_turned", "zT_ready", "lora_mm", "h2_ready",
            "atv_mm", "at_ready", "v1_ready", "sc_mm", "sm_ready", "smax_ready", "nmax_ready", "prob_ready",
            "prob_turned", "probT_ready", "pv_mm", "prec_ready", "h3_ready", "xd_ready", "xr_ready",
            "xk_ready", "rk_mm", "rt_ready", "krelu_ready", "kact_ready", "kv_mm", "rkv_ready", "out_ready",
        ]}
        w_loaded = {n: sem(n + "_loaded") for n in names}
        x_loaded = [sem(f"x_loaded{u}") for u in range(U)]
        out_stored = [sem(f"out_stored{u}") for u in range(U)]

        TOK_BANK, LN0_BANK, V_BANK = [0, 1, 2], [3, 0, 1], [2, 3, 0]

        def tr(n, u):
            b = LN0_BANK[u] if n == 0 else FB + u
            return bank[b][:, 0:KT * T[u]].rearrange("p (k t) -> p k t", k=KT)

        block = ctx.enter_context(nc.Block())

        def run(eng, steps, body):
            body = body.split()

            def call(name, i):
                steps[name[:-1].rstrip(".")](i, int(name[-1]))

            for name in body:
                if name[0] == "F":
                    if name == "F_k0" and "W_G" in steps:
                        steps["W_G"](0, 0)
                    call(name, 0)
            with eng.Fori(1, STEPS) as i:
                for name in body:
                    call(name, i if name[0] == "F" else i - 1)
            for name in body:
                if name[0] == "B":
                    call(name, STEPS - 1)

        @block.sync
        def _(sp):
            def load_x(i, u):
                sp.dma_start(xT[:, :, OFF[u]:OFF[u] + T[u]],
                             a["x"][bass.ds(i * P, P), :, OFF[u]:OFF[u] + T[u]]).then_inc(x_loaded[u], 16)

            def load_w(n, dst, signal):
                sp.dma_start(dst, a[n].rearrange("(t p) n -> p t n", p=P)).then_inc(signal, 16)

            load_w("L0_tok_W_proj", wp_raw, s["wp_loaded"])
            for u in range(U):
                load_x(0, u)
            for n in SPLIT:
                load_w(n, w_raw[n], w_loaded[n])
            load_w(names[3], wT[names[3]][:, :, :], w_loaded[names[3]])
            load_w("L0_ffn_cat", wcat[:, :, :], s["cat_loaded"])
            sp.dma_start(loraB[0:NE * R, :], a["L0_ffn_lora_B"]).then_inc(s["lora_loaded"], 16)
            for n in names[4:]:
                load_w(n, wT[n][:, :, :], w_loaded[n])

            def store(i):
                for u in range(U):
                    sp.wait_ge(s["out_ready"], U * i + u + 1)
                    sp.dma_start(out[bass.ds(i * STOK + OFF[u], T[u]), :],
                                 o_sb[0:T[u], u, :]).then_inc(out_stored[u], 16)

            def fetch(i):
                for u in range(U):
                    sp.wait_ge(s["x_lo_ready"], U * (i - 1) + u + 1)
                    load_x(i, u)

            fetch(1)
            with sp.Fori(1, STEPS - 1) as i:
                fetch(i + 1)
                store(i - 1)
            store(STEPS - 2)
            store(STEPS - 1)
            for u in range(U):
                sp.wait_ge(out_stored[u], 16 * STEPS + 1)

        @block.gpsimd
        def _(pool):
            def row(dst, n):
                v = a[n].rearrange("(o n) -> o n", o=1)
                pool.dma_start(dst, v.to_broadcast([TMAX, v.shape[1]])).then_inc(s["rows_loaded"], 16)

            nc.gpsimd.memset(ident[:, :], 0.0).then_inc(s["const_step"], 1)
            pool.wait_ge(s["const_step"], 1)
            nc.gpsimd.affine_select(ident[:, :], ident[:, :], pattern=[[-1, P]], compare_op=ALU.not_equal,
                                    fill=1.0, base=0, channel_multiplier=1).then_inc(s["ident_ready"], 1)
            for k in range(3):
                pool.dma_start(pos[k * NTOK:(k + 1) * NTOK, :], a["L0_tok_pos_emb"]).then_inc(s["pos_loaded"], 16)
            row(bproj[:, :], "L0_tok_b_proj")
            row(bv[:, :], "L0_attn_bv")
            row(bo[:, :], "L0_attn_bo")
            row(baseb[:, :], "L0_ffn_base_b")
            row(routb[:, :], "L0_ffn_router_b")
            with nc.allow_non_contiguous_dma("per-feature vectors, four bytes a partition"):
                for dst, n in ((bq, "L0_attn_bq"), (bk, "L0_attn_bk"), (mur, "L1_ffn_mu_r"), (muk, "L1_ffn_mu_k")):
                    pool.dma_start(dst[:, :], a[n].rearrange("(t p) -> p t", p=P)).then_inc(s["vecs_loaded"], 16)
            c = [1]

            def link(ins):
                ins.then_inc(s["const_step"], 1)
                c[0] += 1
                pool.wait_ge(s["const_step"], c[0])

            nc.gpsimd.memset(mhalf[:, :], -0.5)
            nc.gpsimd.memset(mask01[:, :], 1.0)
            nc.gpsimd.memset(maskadd[:, :], 0.0)
            nc.gpsimd.memset(headmask[:, :], 1.0)
            link(nc.gpsimd.memset(blockones[:, :], 1.0))
            m01 = mask01[:, :].rearrange("p (b t) -> p b t", b=3)
            mad = maskadd[:, :].rearrange("p (b t) -> p b t", b=3)
            bl = blockones[:, :].rearrange("p (h d) -> p h d", h=HPT)
            hd = headmask[:, :]
            nc.gpsimd.affine_select(m01, m01, pattern=[[NTOK, 3], [1, NTOK]], compare_op=ALU.is_ge, fill=0.0,
                                    base=0, channel_multiplier=-1)
            nc.gpsimd.affine_select(mad, mad, pattern=[[-NTOK, 3], [-1, NTOK]], compare_op=ALU.is_ge, fill=NEG,
                                    base=0, channel_multiplier=1)
            nc.gpsimd.affine_select(hd, hd, pattern=[[-DH, HPT]], compare_op=ALU.is_ge, fill=0.0,
                                    base=0, channel_multiplier=1)
            link(nc.gpsimd.affine_select(bl, bl, pattern=[[-DH, HPT], [0, DH]], compare_op=ALU.is_ge, fill=0.0,
                                         base=0, channel_multiplier=1))
            nc.gpsimd.affine_select(m01, m01, pattern=[[-NTOK, 3], [0, NTOK]], compare_op=ALU.is_ge, fill=0.0,
                                    base=0, channel_multiplier=1)
            nc.gpsimd.affine_select(mad, mad, pattern=[[NTOK, 3], [0, NTOK]], compare_op=ALU.is_ge, fill=NEG,
                                    base=NTOK - 1, channel_multiplier=-1)
            nc.gpsimd.affine_select(hd, hd, pattern=[[DH, HPT]], compare_op=ALU.is_ge, fill=0.0,
                                    base=DH - 1, channel_multiplier=-1)
            nc.gpsimd.affine_select(bl, bl, pattern=[[DH, HPT], [0, DH]], compare_op=ALU.is_ge, fill=0.0,
                                    base=DH - 1, channel_multiplier=-1).then_inc(s["masks_ready"], 1)
            pool.wait_ge(s["pos_loaded"], 48)
            pool.wait_ge(s["rows_loaded"], 16 * 5)
            nc.gpsimd.tensor_tensor(pos[:, :], pos[:, :], bproj[:, :], ALU.add).then_inc(s["pos_ready"], 1)

            def rstd(n, i, u):
                L, t, c = ln[n], T[u], U * i + u + 1
                pool.wait_ge(L.pre_done, c)
                nc.gpsimd.tensor_tensor(L.rs[0:t, u:u + 1], L.ve[0:t, u:u + 1], mhalf[0:t, :],
                                        ALU.pow).then_inc(L.rstd_done, 1)
                pool.wait_ge(L.rstd_done, 2 * U * i + 2 * u + 1)
                nc.gpsimd.tensor_tensor(L.nb[0:t, u:u + 1], L.nm[0:t, u:u + 1], L.rs[0:t, u:u + 1],
                                        ALU.mult).then_inc(L.rstd_done, 1)

            def f_x(i, u):
                o, t = OFF[u], T[u]
                pool.wait_ge(s["x_hi_ready"], U * i + u + 1)
                nc.gpsimd.tensor_tensor(x_lo[:, :, o:o + t], xT[:, :, o:o + t], x_hi[:, :, o:o + t].bitcast(F32),
                                        ALU.subtract).then_inc(s["x_lo_ready"], 1)

            def f_hbo(i, u):
                nc.gpsimd.tensor_tensor(hbo[0:T[u], u, :], hF[0:T[u], u, :], bo[0:T[u], :],
                                        ALU.add).then_inc(s["hbo_ready"], 1)

            def f_hbb(i, u):
                nc.gpsimd.tensor_tensor(hbb[0:T[u], u, :], hB[0:T[u], u, :], baseb[0:T[u], :],
                                        ALU.add).then_inc(s["hbb_ready"], 1)

            def b_xd(i, u):
                n = IMGS[u]
                pool.wait_ge(ln[3].xnT_ready, KT * (U * i + u + 1))
                for k in range(KT):
                    ins = nc.gpsimd.tensor_tensor(xd[:, u, k, 0:T[u]].rearrange("p (b t) -> p b t", b=n),
                                                  xs[:, u, k, 0:n, 1:NTOK + 1], xs[:, u, k, 0:n, 0:NTOK],
                                                  ALU.subtract)
                ins.then_inc(s["xd_ready"], 1)

            def spread(i, j):
                u, ft = j // KT, j % KT
                o, t = OFF[u], T[u]
                pool.wait_ge(s["qT_ready"], KT * i + ft + 1)
                nc.gpsimd.tensor_tensor(
                    qexp[:, ft, :, o:o + t], qT[:, ft:ft + 1, o:o + t].to_broadcast([P, HPT, t]),
                    headmask[:, :].rearrange("p (h o) -> p h o", o=1).to_broadcast([P, HPT, t]),
                    ALU.mult).then_inc(s["qexp_pool"], 1)

            run(pool, {"F_x": f_x, "F_hbo": f_hbo, "F_hbb": f_hbb, "F_spread": spread, "B_xd": b_xd,
                       "F_rs0": lambda i, u: rstd(0, i, u), "F_rs1": lambda i, u: rstd(1, i, u),
                       "B_rs2": lambda i, u: rstd(2, i, u), "B_rs3": lambda i, u: rstd(3, i, u)},
                POOL_BODY)

        @block.tensor
        def _(pe):
            def w_g(i, u):
                qw, kw = wT["L1_attn_Qw"], wT["L1_attn_Kw"]
                pe.wait_ge(w_loaded["L1_attn_Qw"], 16)
                pe.wait_ge(w_loaded["L1_attn_Kw"], 16)
                for ft in range(KT):
                    for dt in range(KT):
                        ins = nc.tensor.matmul(bank[7][:, ft * E:(ft + 1) * E], qw[:, dt, ft * P:(ft + 1) * P],
                                               kw[:, dt, :], start=(dt == 0), stop=(dt == KT - 1))
                ins.then_inc(s["g_mm"], 1)
                for n in names[6:]:
                    pe.wait_ge(w_loaded[n], 16)
                pe.wait_ge(s["cat_loaded"], 16)
                pe.wait_ge(s["lora_loaded"], 16)
                pe.wait_ge(s["zeros_ready"], 1)
                pe.wait_ge(s["g_ready"], 1)

            def product3(out_ap, pairs):
                terms = [(a[x], b[y]) for a, b in pairs for x, y in ((0, 0), (0, 1), (1, 0))]
                for n, (lhs, rhs) in enumerate(terms):
                    ins = nc.tensor.matmul(out_ap, lhs, rhs, start=(n == 0), stop=(n == len(terms) - 1))
                return ins

            def f_tok(i, u):
                o, t = OFF[u], T[u]
                if isinstance(i, int):
                    pe.wait_ge(s["wp_hi_ready"], 1)
                    pe.wait_ge(s["wp_lo_ready"], 1)
                pe.wait_ge(s["x_hi_ready"], U * i + u + 1)
                pe.wait_ge(s["x_lo_ready"], U * i + u + 1)
                product3(bank[TOK_BANK[u]][0:t, 0:E],
                         [((x_hi[:, c, o:o + t], x_lo[:, c, o:o + t]), (wp_hi[:, c, :], wp_lo[:, c, :]))
                          for c in range(KC)]).then_inc(s["tok_mm"], 1)

            def turn_ln(n):
                def step(i, u):
                    pe.wait_ge(ln[n].xn_done, U * i + u + 1)
                    for k in range(KT):
                        ins = nc.tensor.transpose(tr(n, u)[:, k, :], ln[n].xn[0:T[u], u, k * P:(k + 1) * P],
                                                  ident[0:T[u], 0:T[u]])
                    ins.then_inc(ln[n].turned, 1)
                return step

            def wide(w, ft, b, done):
                product3(bank[b][:, 0:STOK],
                         [((w_hi[w][:, k, ft * P:(ft + 1) * P], w_lo[w][:, k, ft * P:(ft + 1) * P]),
                           (xn0_hi[:, k, :], xn0_lo[:, k, :])) for k in range(KT)]).then_inc(s[done], 1)

            def f_k(i, ft):
                if ft == 0:
                    pe.wait_ge(ln[0].xnT_ready, U * i + U)
                    pe.wait_ge(s["xn0_lo_ready"], U * i + U)
                    if isinstance(i, int):
                        pe.wait_ge(s["w_hi_ready"], len(SPLIT))
                        pe.wait_ge(s["w_lo_ready"], len(SPLIT))
                wide("L0_attn_Wk", ft, [3, 0][ft], "k_mm")

            def f_v(i, u):
                o, t, w = OFF[u], T[u], "L0_attn_Wv"
                if u:
                    pe.wait_ge(s["kT_ready"], KT * i + u)
                product3(bank[V_BANK[u]][0:t, 0:E],
                         [((xn0_hi[:, k, o:o + t], xn0_lo[:, k, o:o + t]), (w_hi[w][:, k, :], w_lo[w][:, k, :]))
                          for k in range(KT)]).then_inc(s["v_mm"], 1)

            def f_q(i, ft):
                wide("L0_attn_Wq", ft, [4, 1][ft], "q_mm")

            SB = [2, 3, 0]

            def f_sc(i, ju):
                u, ft = ju // KT, ju % KT
                if u == 0:
                    pe.wait_ge(s["qexp_ready"], KT * i + ft + 1)
                else:
                    pe.wait_ge(s["qexp_pool"], KT * (U - 1) * i + ju - KT + 1)
                for half in range(2):
                    j = 2 * ju + half
                    if j == 0:
                        pe.wait_ge(s["kT_ready"], KT * i + KT)
                    if j < 3:
                        pe.wait_ge(s["vpad_ready"], U * i + j + 1)
                    if j >= 3:
                        pe.wait_ge(s["s_masked"], 12 * i + j - 2)
                    nc.tensor.matmul(
                        bank[SB[j % 3]][0:T[u], 0:4 * T[u]].rearrange("p (h t) -> p h t", h=4),
                        kT[:, ft, OFF[u]:OFF[u] + T[u]],
                        qexp[:, ft, 4 * half:4 * half + 4, OFF[u]:OFF[u] + T[u]],
                        start=True, stop=True).then_inc(s["s_mm"], 1)

            def f_den(i, ft):
                pe.wait_ge(s["qk_ready"], KT * i + ft + 1)
                nc.tensor.matmul(bank[[4, 1][ft]][:, 0:STOK], blockones[:, :], qk[:, ft, :],
                                 start=True, stop=True).then_inc(s["den_mm"], 1)

            def f_av(i, u):
                pe.wait_ge(s["s_masked"], 12 * i + 4 * u + 4)
                if u == 0:
                    pe.wait_ge(s["den_floor"], KT * i + KT)
                else:
                    pe.wait_ge(s["attnT_ready"], U * i + u)
                for ft in range(KT):
                    for e in range(2):
                        for r in range(4):
                            pair = 4 * ft + r
                            ins = nc.tensor.matmul(
                                bank[1][32 * r:32 * r + 32, ft * T[u]:(ft + 1) * T[u]],
                                vpad[0:T[u], u, pair, e, :, :].rearrange("p a d -> p (a d)"),
                                S[0:T[u], u, 2 * pair + e, 0:T[u]], start=(e == 0), stop=(e == 1),
                                tile_position=(0, 32 * r))
                ins.then_inc(s["av_mm"], 1)

            def project(b, t, lhs, w, done):
                for k in range(KT):
                    ins = nc.tensor.matmul(bank[b][0:t, 0:w.shape[2]], lhs(k), w[:, k, :],
                                           start=(k == 0), stop=(k == KT - 1))
                ins.then_inc(s[done], 1)

            def f_wo(i, u):
                pe.wait_ge(s["attnT_ready"], U * i + u + 1)
                if u == 0:
                    if isinstance(i, int):
                        pe.wait_ge(w_loaded["L0_attn_Wo"], 16)
                else:
                    pe.wait_ge(s["h1_ready"], U * i + u)
                project(4, T[u], lambda k: attnT[:, u, k, 0:T[u]], wT["L0_attn_Wo"], "wo_mm")

            def b_ffn(i, u):
                pe.wait_ge(ln[1].xnT_ready, U * i + u + 1)
                project(FB + u, T[u], lambda k: ln[1].xnT[:, k, OFF[u]:OFF[u] + T[u]], wcat, "ffn_mm")

            def b_z(i, u):
                pe.wait_ge(s["z_ready"], U * i + u + 1)
                pe.wait_ge(s["h2a_ready"], U * i + u + 1)
                nc.tensor.transpose(bank[FB + u][:, 0:T[u]], z[0:T[u], u, :],
                                    ident[0:T[u], 0:T[u]]).then_inc(s["z_turned"], 1)

            def b_lora(i, u):
                pe.wait_ge(s["zT_ready"], U * i + u + 1)
                nc.tensor.matmul(bank[FB + u][0:T[u], 0:E], zT[:, u, 0:T[u]], loraB[:, :],
                                 start=True, stop=True).then_inc(s["lora_mm"], 1)

            def b_atv(i, u):
                pe.wait_ge(ln[2].xnT_ready, U * i + u + 1)
                for ft in range(KT):
                    for k in range(KT):
                        nc.tensor.matmul(bank[FB + u][:, ft * T[u]:(ft + 1) * T[u]],
                                         G[:, k, ft * P:(ft + 1) * P], ln[2].xnT[:, k, OFF[u]:OFF[u] + T[u]],
                                         start=(k == 0), stop=(k == KT - 1))
                for k in range(KT):
                    ins = nc.tensor.matmul(bank[FB + u][0:T[u], E:2 * E], ln[2].xnT[:, k, OFF[u]:OFF[u] + T[u]],
                                           wT["L1_attn_Vw"][:, k, :], start=(k == 0), stop=(k == KT - 1))
                ins.then_inc(s["atv_mm"], 1)

            def b_sc(i, u):
                pe.wait_ge(s["at_ready"], U * i + u + 1)
                pe.wait_ge(s["v1_ready"], U * i + u + 1)
                for k in range(KT):
                    ins = nc.tensor.matmul(bank[FB + u][0:T[u], 0:T[u]], at[:, u, k, 0:T[u]],
                                           ln[2].xnT[:, k, OFF[u]:OFF[u] + T[u]],
                                           start=(k == 0), stop=(k == KT - 1))
                ins.then_inc(s["sc_mm"], 1)

            def b_pt(i, u):
                pe.wait_ge(s["prob_ready"], U * i + u + 1)
                nc.tensor.transpose(bank[FB + u][0:T[u], 0:T[u]], prob[0:T[u], u, 0:T[u]],
                                    ident[0:T[u], 0:T[u]]).then_inc(s["prob_turned"], 1)

            def b_pv(i, u):
                pe.wait_ge(s["probT_ready"], U * i + u + 1)
                nc.tensor.matmul(bank[FB + u][0:T[u], 0:E], probT[0:T[u], u, 0:T[u]], v1[0:T[u], u, :],
                                 start=True, stop=True).then_inc(s["pv_mm"], 1)

            def b_rk(i, u):
                pe.wait_ge(s["xr_ready"], U * i + u + 1)
                for k in range(KT):
                    nc.tensor.matmul(bank[FB + u][0:T[u], 0:E], xr[:, u, k, 0:T[u]],
                                     wT["L1_ffn_W_r"][:, k, :], start=(k == 0), stop=(k == KT - 1))
                pe.wait_ge(s["xk_ready"], U * i + u + 1)
                for ft in range(KT):
                    for k in range(KT):
                        ins = nc.tensor.matmul(bank[FB + u][:, E + ft * T[u]:E + (ft + 1) * T[u]],
                                               wT["L1_ffn_W_k"][:, k, ft * P:(ft + 1) * P],
                                               xk[:, u, k, 0:T[u]], start=(k == 0), stop=(k == KT - 1))
                ins.then_inc(s["rk_mm"], 1)

            def b_out(i, u):
                pe.wait_ge(s["kact_ready"], U * i + u + 1)
                pe.wait_ge(s["rt_ready"], U * i + u + 1)
                project(FB + u, T[u], lambda k: kact[:, u, k, 0:T[u]], wT["L1_ffn_W_v"], "kv_mm")

            pe.wait_ge(s["ident_ready"], 1)
            run(pe, {"F_tok": f_tok, "F_tr0": turn_ln(0), "W_G": w_g, "F_k": f_k, "F_v": f_v, "F_q": f_q,
                     "F_sc": f_sc, "F_den": f_den, "F_av": f_av, "F_wo": f_wo,
                     "B_tr1": turn_ln(1), "B_ffn": b_ffn, "B_z": b_z, "B_lora": b_lora, "B_tr2": turn_ln(2),
                     "B_atv": b_atv, "B_sc": b_sc, "B_pt": b_pt, "B_pv": b_pv, "B_tr3": turn_ln(3),
                     "B_rk": b_rk, "B_out": b_out}, PE_BODY)

        @block.scalar
        def _(act):
            def copy(dst, src):
                return nc.scalar.activation(dst, src, ACT.Copy)

            def w_g(i, u):
                act.wait_ge(s["g_mm"], 1)
                copy(G[:, :, :], bank[7][:, :].rearrange("p (k e) -> p k e", k=KT)).then_inc(s["g_ready"], 1)

            def f_x(i, u):
                o, t = OFF[u], T[u]
                act.wait_ge(x_loaded[u], 16 * i + 16)
                copy(x_hi[:, :, o:o + t], xT[:, :, o:o + t]).then_inc(s["x_hi_ready"], 1)

            def f_x_later(i, u):
                if not isinstance(i, int):
                    f_x(i, u)

            def apply_ln(n, h):
                def step(i, u):
                    L, t = ln[n], T[u]
                    act.wait_ge(L.rstd_done, 2 * (U * i + u + 1))
                    nc.scalar.activation(L.xn[0:t, u, :], h[0:t, u, :], ACT.Identity, bias=L.nb[0:t, u:u + 1],
                                         scale=L.rs[0:t, u:u + 1]).then_inc(L.xn_done, 1)
                return step

            def take_turned(n):
                def step(i, u):
                    act.wait_ge(ln[n].turned, U * i + u + 1)
                    if n == 0:
                        copy(xn0_hi[:, :, OFF[u]:OFF[u] + T[u]], tr(n, u)).then_inc(ln[n].xnT_ready, 1)
                    elif n == 3:
                        for k in range(KT):
                            copy(xs[:, u, k, 0:IMGS[u], 1:NTOK + 1],
                                 tr(n, u)[:, k, :].rearrange("p (b t) -> p b t", b=IMGS[u])
                                 ).then_inc(ln[n].xnT_ready, 1)
                    else:
                        copy(ln[n].xnT[:, :, OFF[u]:OFF[u] + T[u]], tr(n, u)).then_inc(ln[n].xnT_ready, 1)
                return step

            def feature_exp(name, banks, nbias, dst):
                def step(i, ft):
                    act.wait_ge(s[f"{name}_mm"], KT * i + ft + 1)
                    nc.scalar.activation(dst[:, ft, :], bank[banks[ft]][:, 0:STOK], ACT.Relu,
                                         bias=nbias[:, ft:ft + 1], scale=-1.0).then_inc(s[f"{name}_min"], 1)
                    act.wait_ge(s[f"{name}_min"], KT * i + ft + 1)
                    nc.scalar.activation(dst[:, ft, :], dst[:, ft, :], ACT.Exp, scale=-1.0
                                         ).then_inc(s[f"{name}_exp"], 1)
                return step

            def b_ffn(i, u):
                t = T[u]
                act.wait_ge(s["lsub_ready"], U * i + u + 1)
                nc.scalar.activation(lexp[0:t, u, :], lsub[0:t, u, :], ACT.Exp,
                                     accum_out=lsum[0:t, u:u + 1]).then_inc(s["lexp_ready"], 1)

            def b_z(i, u):
                act.wait_ge(s["z_turned"], U * i + u + 1)
                copy(zT[:, u, 0:T[u]], bank[FB + u][:, 0:T[u]]).then_inc(s["zT_ready"], 1)

            def b_atv(i, u):
                t = T[u]
                act.wait_ge(s["atv_mm"], U * i + u + 1)
                copy(at[:, u, :, 0:t], bank[FB + u][:, 0:KT * t].rearrange("p (k t) -> p k t", k=KT)
                     ).then_inc(s["at_ready"], 1)
                copy(v1[0:t, u, :], bank[FB + u][0:t, E:2 * E]).then_inc(s["v1_ready"], 1)

            def b_sc(i, u):
                t = T[u]
                act.wait_ge(s["nmax_ready"], U * i + u + 1)
                nc.scalar.activation(prob[0:t, u, 0:t], sm[0:t, u, 0:t], ACT.Exp, bias=nmax[0:t, u:u + 1],
                                     scale=float(E) ** -0.5, accum_out=psm[0:t, u:u + 1]
                                     ).then_inc(s["prob_ready"], 1)

            def b_pt(i, u):
                act.wait_ge(s["prob_turned"], U * i + u + 1)
                copy(probT[0:T[u], u, 0:T[u]], bank[FB + u][0:T[u], 0:T[u]]).then_inc(s["probT_ready"], 1)

            def b_rk(i, u):
                t = T[u]
                act.wait_ge(s["rk_mm"], U * i + u + 1)
                nc.scalar.activation(kact[:, u, :, 0:t],
                                     bank[FB + u][:, E:E + KT * t].rearrange("p (k t) -> p k t", k=KT),
                                     ACT.Relu).then_inc(s["krelu_ready"], 1)
                nc.scalar.activation(rt[0:t, u, :], bank[FB + u][0:t, 0:E], ACT.Tanh, scale=0.5
                                     ).then_inc(s["rt_ready"], 1)

            act.wait_ge(s["wp_loaded"], 16)
            copy(wp_hi[:, :, :], wp_raw).then_inc(s["wp_hi_ready"], 1)
            for u in range(U):
                f_x(0, u)
            for n in SPLIT:
                act.wait_ge(w_loaded[n], 16)
                copy(w_hi[n][:, :, :], w_raw[n]).then_inc(s["w_hi_ready"], 1)
            act.wait_ge(s["bias1_ready"], 1)
            run(act, {"F_x": f_x_later, "F_ap0": apply_ln(0, hF), "F_ct0": take_turned(0), "W_G": w_g,
                      "F_k": feature_exp("k", (3, 0), nbk, kmin), "F_q": feature_exp("q", (4, 1), nbq, qmin),
                      "F_ap1": apply_ln(1, hB), "B_ct1": take_turned(1), "B_ffn": b_ffn, "B_z": b_z,
                      "B_ap2": apply_ln(2, hB), "B_ct2": take_turned(2),
                      "B_atv": b_atv, "B_sc": b_sc, "B_pt": b_pt, "B_ap3": apply_ln(3, hB),
                      "B_ct3": take_turned(3), "B_rk": b_rk}, ACT_BODY)

        @block.vector
        def _(dve):
            nc.vector.memset(vpad[:, :, :, :, :, :], 0.0)
            nc.vector.memset(z[:, :, :], 0.0)
            for u in range(U):
                nc.vector.memset(o_sb[:, u, 0:1], 0.0).then_inc(out_stored[u], 1)
            nc.vector.memset(xs[:, :, :, :, 0:1], 0.0)
            nc.vector.memset(restart[:, :], 1.0)
            nc.vector.memset(loraB[NE * R:P, :], 0.0).then_inc(s["zeros_ready"], 1)
            dve.wait_ge(s["zeros_ready"], 1)
            rs_v = restart[:, :].rearrange("p (b t) -> p b t", b=STEP_IMGS)
            nc.vector.memset(rs_v[:, :, 0:1], 0.0).then_inc(s["zeros_ready"], 1)
            dve.wait_ge(s["vecs_loaded"], 64)
            nc.vector.tensor_scalar(bk1[:, :], bk[:, :], 1.0, None, ALU.add)
            nc.vector.tensor_scalar(nbk[:, :], bk[:, :], -1.0, None, ALU.mult)
            nc.vector.tensor_scalar(nbq[:, :], bq[:, :], -1.0, None, ALU.mult)
            nc.vector.tensor_scalar(bq1[:, :], bq[:, :], 1.0, None, ALU.add).then_inc(s["bias1_ready"], 1)
            dve.wait_ge(s["bias1_ready"], 1)
            dve.wait_ge(s["zeros_ready"], 2)
            dve.wait_ge(s["wp_hi_ready"], 1)
            nc.vector.tensor_tensor(wp_lo[:, :, :], wp_raw, wp_hi[:, :, :].bitcast(F32),
                                    ALU.subtract).then_inc(s["wp_lo_ready"], 1)
            for j, n in enumerate(SPLIT):
                dve.wait_ge(s["w_hi_ready"], j + 1)
                nc.vector.tensor_tensor(w_lo[n][:, :, :], w_raw[n], w_hi[n][:, :, :].bitcast(F32),
                                        ALU.subtract).then_inc(s["w_lo_ready"], 1)
            dve.wait_ge(s["masks_ready"], 1)
            dve.wait_ge(s["pos_ready"], 1)

            def stats(n, h, h_ready):
                def step(i, u):
                    L, t = ln[n], T[u]
                    dve.wait_ge(h_ready, U * i + u + 1)
                    nc.vector.bn_stats(L.st[0:t, u, :], h[0:t, u, :]).then_inc(L.stats_done, 1)
                return step

            def mean_var(n):
                def step(i, u):
                    L, t = ln[n], T[u]
                    dve.wait_ge(s["pos_ready"], 1)
                    dve.wait_ge(L.stats_done, U * i + u + 1)
                    nc.vector.bn_aggr(L.mv[0:t, u, :], L.st[0:t, u, :]).then_inc(L.var_done, 1)
                return step

            def var_eps(n):
                def step(i, u):
                    L, t = ln[n], T[u]
                    dve.wait_ge(L.var_done, U * i + u + 1)
                    nc.vector.tensor_scalar(L.ve[0:t, u:u + 1], L.mv[0:t, u, 1:2], LN_EPS, None, ALU.add)
                    nc.vector.tensor_scalar(L.nm[0:t, u:u + 1], L.mv[0:t, u, 0:1], -1.0, None,
                                            ALU.mult).then_inc(L.pre_done, 1)
                return step

            def f_tok(i, u):
                t = T[u]
                dve.wait_ge(s["tok_mm"], U * i + u + 1)
                nc.vector.tensor_tensor(hF[0:t, u, :], bank[TOK_BANK[u]][0:t, 0:E], pos[0:t, :],
                                        ALU.add).then_inc(s["hF_ready"], 1)

            def f_tr(i, u):
                o, t = OFF[u], T[u]
                dve.wait_ge(ln[0].xnT_ready, U * i + u + 1)
                nc.vector.tensor_tensor(xn0_lo[:, :, o:o + t], tr(0, u), xn0_hi[:, :, o:o + t].bitcast(F32),
                                        ALU.subtract).then_inc(s["xn0_lo_ready"], 1)

            def feature(name, banks, bias1, src, dst):
                def step(i, ft):
                    dve.wait_ge(s[f"{name}_exp"], KT * i + ft + 1)
                    nc.vector.scalar_tensor_tensor(out=dst[:, ft, :], in0=bank[banks[ft]][:, 0:STOK],
                                                   scalar=bias1[:, ft:ft + 1], in1=src[:, ft, :],
                                                   op0=ALU.add, op1=ALU.max).then_inc(s[f"{name}T_ready"], 1)
                return step

            feature_k = feature("k", (3, 0), bk1, kmin, kT)
            feature_q = feature("q", (4, 1), bq1, qmin, qT)

            def f_v(i, u):
                t, b = T[u], V_BANK[u]
                dve.wait_ge(s["v_mm"], U * i + u + 1)
                for e in range(2):
                    ins = nc.vector.tensor_tensor(
                        vpad[0:t, u, :, e, e, :],
                        bank[b][0:t, 0:E].rearrange("p (j e d) -> p j e d", e=2, d=DH)[:, :, e, :],
                        bv[0:t, :].rearrange("p (j e d) -> p j e d", e=2, d=DH)[:, :, e, :], ALU.add)
                ins.then_inc(s["vpad_ready"], 1)

            def f_cum(i, ft):
                dve.wait_ge(s["kT_ready"], KT * i + ft + 1)
                nc.vector.tensor_tensor_scan(kcum[:, ft, :], restart[:, :], kT[:, ft, :], 0.0,
                                             ALU.mult, ALU.add).then_inc(s["kcum_ready"], 1)

            def f_spread(i, ft):
                t = T[0]
                dve.wait_ge(s["qT_ready"], KT * i + ft + 1)
                nc.vector.tensor_tensor(
                    qexp[:, ft, :, 0:t], qT[:, ft:ft + 1, 0:t].to_broadcast([P, HPT, t]),
                    headmask[:, :].rearrange("p (h o) -> p h o", o=1).to_broadcast([P, HPT, t]),
                    ALU.mult).then_inc(s["qexp_ready"], 1)

            def f_qk(i, ft):
                dve.wait_ge(s["qT_ready"], KT * i + ft + 1)
                dve.wait_ge(s["kcum_ready"], KT * i + ft + 1)
                nc.vector.tensor_tensor(qk[:, ft, :], qT[:, ft, :], kcum[:, ft, :],
                                        ALU.mult).then_inc(s["qk_ready"], 1)

            def f_sc(i, ju):
                u = ju // KT
                t = T[u]
                for half in range(2):
                    j = 2 * ju + half
                    j4 = j - 4 * u
                    dve.wait_ge(s["s_mm"], 12 * i + j + 1)
                    nc.vector.tensor_tensor(
                        S[0:t, u, 4 * j4:4 * j4 + 4, 0:t],
                        bank[[2, 3, 0][j % 3]][0:t, 0:4 * t].rearrange("p (h t) -> p h t", h=4),
                        mask01[0:t, 0:t].rearrange("p (o t) -> p o t", o=1).to_broadcast([t, 4, t]),
                        ALU.mult).then_inc(s["s_masked"], 1)

            def f_fl(i, ft):
                dve.wait_ge(s["den_mm"], KT * i + ft + 1)
                nc.vector.tensor_scalar(rden[:, ft, :], bank[[4, 1][ft]][:, 0:STOK], DEN_EPS, None,
                                        ALU.max).then_inc(s["den_floor"], 1)

            def f_rc(i, ft):
                dve.wait_ge(s["den_floor"], KT * i + ft + 1)
                nc.vector.reciprocal(rden[:, ft, :], rden[:, ft, :]).then_inc(s["rden_ready"], 1)

            def f_av(i, u):
                o, t = OFF[u], T[u]
                dve.wait_ge(s["rden_ready"], KT * i + KT)
                dve.wait_ge(s["av_mm"], U * i + u + 1)
                nc.vector.tensor_tensor(attnT[:, u, :, 0:t],
                                        bank[1][:, 0:KT * t].rearrange("p (k t) -> p k t", k=KT),
                                        rden[:, :, o:o + t], ALU.mult).then_inc(s["attnT_ready"], 1)

            def f_wo(i, u):
                t = T[u]
                dve.wait_ge(s["wo_mm"], U * i + u + 1)
                dve.wait_ge(s["hbo_ready"], U * i + u + 1)
                if not isinstance(i, int):
                    dve.wait_ge(s["out_ready"], U * (i - 1) + u + 1)
                nc.vector.tensor_tensor(hB[0:t, u, :], bank[4][0:t, 0:E], hbo[0:t, u, :],
                                        ALU.add).then_inc(s["h1_ready"], 1)

            def b_ffn(i, u):
                t, b, c = T[u], FB + u, U * i + u + 1
                dve.wait_ge(s["ffn_mm"], c)
                nc.vector.tensor_tensor(logit[0:t, u, :], bank[b][0:t, E:E + NE], routb[0:t, :],
                                        ALU.add).then_inc(s["logit_ready"], 1)
                nc.vector.tensor_scalar(mid[0:t, u, :], bank[b][0:t, E + NE:NCAT], LORA_SCALING, None,
                                        ALU.mult).then_inc(s["mid_ready"], 1)

            def b_lmax(i, u):
                t, c = T[u], U * i + u + 1
                dve.wait_ge(s["logit_ready"], c)
                nc.vector.tensor_reduce(lmax[0:t, u:u + 1], logit[0:t, u, :], AX, ALU.max
                                        ).then_inc(s["lmax_ready"], 1)

            def b_lsub(i, u):
                t, c = T[u], U * i + u + 1
                dve.wait_ge(s["lmax_ready"], c)
                nc.vector.tensor_scalar(lsub[0:t, u, :], logit[0:t, u, :], lmax[0:t, u:u + 1], None,
                                        ALU.subtract).then_inc(s["lsub_ready"], 1)

            def b_h2a(i, u):
                t, b, c = T[u], FB + u, U * i + u + 1
                dve.wait_ge(s["hbb_ready"], c)
                dve.wait_ge(s["ffn_mm"], c)
                nc.vector.tensor_tensor(hB[0:t, u, :], bank[b][0:t, 0:E], hbb[0:t, u, :],
                                        ALU.add).then_inc(s["h2a_ready"], 1)

            def b_lrec(i, u):
                t, c = T[u], U * i + u + 1
                dve.wait_ge(s["lexp_ready"], c)
                nc.vector.reciprocal(lrec[0:t, u:u + 1], lsum[0:t, u:u + 1]).then_inc(s["lrec_ready"], 1)

            def b_gate(i, u):
                t, c = T[u], U * i + u + 1
                dve.wait_ge(s["lrec_ready"], c)
                nc.vector.tensor_scalar(gate[0:t, u, :], lexp[0:t, u, :], lrec[0:t, u:u + 1], None,
                                        ALU.mult).then_inc(s["gate_ready"], 1)

            def b_z(i, u):
                t, c = T[u], U * i + u + 1
                dve.wait_ge(s["gate_ready"], c)
                dve.wait_ge(s["mid_ready"], c)
                nc.vector.tensor_tensor(
                    z[0:t, u, 0:NE * R].rearrange("p (e r) -> p e r", e=NE),
                    gate[0:t, u, :].rearrange("p (e o) -> p e o", o=1).to_broadcast([t, NE, R]),
                    mid[0:t, u:u + 1, :].to_broadcast([t, NE, R]), ALU.mult).then_inc(s["z_ready"], 1)

            def b_lora(i, u):
                t, c = T[u], U * i + u + 1
                dve.wait_ge(s["lora_mm"], c)
                dve.wait_ge(s["h2a_ready"], c)
                nc.vector.tensor_tensor(hB[0:t, u, :], bank[FB + u][0:t, 0:E], hB[0:t, u, :],
                                        ALU.add).then_inc(s["h2_ready"], 1)

            def b_sc(i, u):
                t, c = T[u], U * i + u + 1
                dve.wait_ge(s["sc_mm"], c)
                nc.vector.tensor_tensor(sm[0:t, u, 0:t], bank[FB + u][0:t, 0:t], maskadd[0:t, 0:t],
                                        ALU.add).then_inc(s["sm_ready"], 1)

            def b_smax(i, u):
                t, c = T[u], U * i + u + 1
                dve.wait_ge(s["sm_ready"], c)
                nc.vector.tensor_reduce(smax[0:t, u:u + 1], sm[0:t, u, 0:t], AX, ALU.max
                                        ).then_inc(s["smax_ready"], 1)

            def b_nmax(i, u):
                t, c = T[u], U * i + u + 1
                dve.wait_ge(s["smax_ready"], c)
                nc.vector.tensor_scalar(nmax[0:t, u:u + 1], smax[0:t, u:u + 1], -float(E) ** -0.5, None,
                                        ALU.mult).then_inc(s["nmax_ready"], 1)

            def b_prec(i, u):
                t, c = T[u], U * i + u + 1
                dve.wait_ge(s["prob_ready"], c)
                nc.vector.reciprocal(prec[0:t, u:u + 1], psm[0:t, u:u + 1]).then_inc(s["prec_ready"], 1)

            def b_pv(i, u):
                t, c = T[u], U * i + u + 1
                dve.wait_ge(s["prec_ready"], c)
                dve.wait_ge(s["pv_mm"], c)
                nc.vector.scalar_tensor_tensor(out=hB[0:t, u, :], in0=bank[FB + u][0:t, 0:E],
                                               scalar=prec[0:t, u:u + 1], in1=hB[0:t, u, :],
                                               op0=ALU.mult, op1=ALU.add).then_inc(s["h3_ready"], 1)

            def mix(name, dst, mu):
                def step(i, u):
                    n = IMGS[u]
                    dve.wait_ge(s["xd_ready"], U * i + u + 1)
                    for k in range(KT):
                        ins = nc.vector.scalar_tensor_tensor(
                            out=dst[:, u, k, 0:T[u]].rearrange("p (b t) -> p b t", b=n),
                            in0=xd[:, u, k, 0:T[u]].rearrange("p (b t) -> p b t", b=n), scalar=mu[:, k:k + 1],
                            in1=xs[:, u, k, 0:n, 0:NTOK], op0=ALU.mult, op1=ALU.add)
                    ins.then_inc(s[name], 1)
                return step

            def b_rk(i, u):
                t = T[u]
                dve.wait_ge(s["krelu_ready"], U * i + u + 1)
                nc.vector.tensor_tensor(kact[:, u, :, 0:t], kact[:, u, :, 0:t], kact[:, u, :, 0:t],
                                        ALU.mult).then_inc(s["kact_ready"], 1)

            def b_rkv(i, u):
                t, c = T[u], U * i + u + 1
                dve.wait_ge(s["kv_mm"], c)
                dve.wait_ge(s["rt_ready"], c)
                nc.vector.scalar_tensor_tensor(out=rt[0:t, u, :], in0=rt[0:t, u, :], scalar=1.0,
                                               in1=bank[FB + u][0:t, 0:E], op0=ALU.add, op1=ALU.mult
                                               ).then_inc(s["rkv_ready"], 1)

            def b_out(i, u):
                t, c = T[u], U * i + u + 1
                dve.wait_ge(s["rkv_ready"], c)
                dve.wait_ge(out_stored[u], 16 * i + 1)
                nc.vector.scalar_tensor_tensor(out=o_sb[0:t, u, :], in0=rt[0:t, u, :], scalar=0.5,
                                               in1=hB[0:t, u, :], op0=ALU.mult, op1=ALU.add
                                               ).then_inc(s["out_ready"], 1)

            run(dve, {"F_tok": f_tok, "F_lo": f_tr, "F_v": f_v, "F_k": feature_k, "F_cum": f_cum,
                      "F_q": feature_q, "F_spr": f_spread, "F_qk": f_qk, "F_sc": f_sc, "F_fl": f_fl,
                      "F_rc": f_rc, "F_av": f_av, "F_wo": f_wo,
                      "F_st0": stats(0, hF, s["hF_ready"]), "F_mv0": mean_var(0), "F_ve0": var_eps(0),
                      "F_st1": stats(1, hB, s["h1_ready"]), "F_mv1": mean_var(1), "F_ve1": var_eps(1),
                      "B_st2": stats(2, hB, s["h2_ready"]), "B_mv2": mean_var(2), "B_ve2": var_eps(2),
                      "B_st3": stats(3, hB, s["h3_ready"]), "B_mv3": mean_var(3), "B_ve3": var_eps(3),
                      "B_ffn": b_ffn, "B_lmax": b_lmax, "B_lsub": b_lsub, "B_h2a": b_h2a, "B_lrec": b_lrec,
                      "B_gate": b_gate, "B_z": b_z, "B_lora": b_lora, "B_sc": b_sc, "B_smax": b_smax,
                      "B_nmax": b_nmax, "B_prec": b_prec, "B_pv": b_pv, "B_xr": mix("xr_ready", xr, mur),
                      "B_xk": mix("xk_ready", xk, muk), "B_rk": b_rk, "B_rkv": b_rkv, "B_out": b_out},
                DVE_BODY)


def kernel(**inputs):
    import numpy as _np
    import concourse.bacc as _bacc
    from concourse import mybir as _mybir
    from concourse.bass_utils import run_bass_kernel_spmd as _run

    host = {n: _np.asarray(v) for n, v in inputs.items()}
    x = host["x"].reshape(B, GRID, PATCH, GRID, PATCH, C).transpose(0, 1, 3, 2, 4, 5)
    x = x.reshape(STEPS, STOK, KC, P).transpose(0, 3, 2, 1).reshape(STEPS * P, KC, STOK)
    laid = {"x": x}
    for n in ("L0_tok_W_proj", "L0_attn_Wk", "L0_attn_Wv", "L0_attn_Wq", "L0_attn_Wo", "L1_attn_Qw", "L1_attn_Kw",
              "L1_ffn_W_r", "L1_ffn_W_k", "L1_ffn_W_v"):
        laid[n] = host[n].T
    laid["L0_ffn_cat"] = _np.concatenate([host["L0_ffn_base_w"].T, host["L0_ffn_router_w"].T,
                                          host["L0_ffn_lora_A"]], axis=1)
    laid["L0_ffn_lora_B"] = host["L0_ffn_lora_B"].reshape(NE * R, E)
    for n in ("L1_attn_Vw", "L0_tok_b_proj", "L0_tok_pos_emb", "L0_attn_bq", "L0_attn_bk", "L0_attn_bv", "L0_attn_bo",
              "L0_ffn_base_b", "L0_ffn_router_b", "L1_ffn_mu_r", "L1_ffn_mu_k"):
        laid[n] = host[n]

    nc = _bacc.Bacc("TRN2", target_bir_lowering=False, num_devices=1)
    arrays, args = {}, {}
    for name, v in laid.items():
        v = _np.ascontiguousarray(v)
        arrays[f"in_{name}_dram"] = v
        args[name] = nc.dram_tensor(f"in_{name}_dram", v.shape, _mybir.dt.from_np(v.dtype), kind="ExternalInput").ap()
    args["out"] = nc.dram_tensor("out_0_dram", (B, NTOK, E), F32, kind="ExternalOutput").ap()
    vit_tower_kernel(nc, args)
    r = _run(nc, [arrays], core_ids=[0])
    return r.results[0]["out_0_dram"]
```

```python
from contextlib import ExitStack

import concourse.bass as bass
from concourse import mybir

F32 = mybir.dt.float32
BF16 = mybir.dt.bfloat16
F32R = mybir.dt.float32r
ALU = mybir.AluOpType
ACT = mybir.ActivationFunctionType
AX = mybir.AxisListType.X

P = 128
B, HW, C = 32, 96, 3
PATCH = 16
GRID = HW // PATCH
NTOK = GRID * GRID
PD = PATCH * PATCH * C
KC = PD // P
E = 256
KT = E // P
NH, DH = 16, 16
HPT = P // DH
NE, R = 8, 8
LORA_SCALING = 16.0 / R
LN_EPS = 1e-5
DEN_EPS = 1e-6
STEP_IMGS = 8
STEPS = B // STEP_IMGS
STOK = STEP_IMGS * NTOK
IMGS = [3, 3, 2]
U = len(IMGS)
T = [n * NTOK for n in IMGS]
OFF = [0, T[0], T[0] + T[1]]
TMAX = max(T)
NEG = -1e30
FB = 5


PE_BODY = """
    B_tr1.0 F_k0 F_k1 F_q0 B_tr1.1 F_q1 B_tr1.2 B_ffn0 B_ffn1 B_ffn2 P_tok0 B_z0 B_z1 F_v0 B_lora0
    B_lora1 F_v1 P_tok1 B_z2 F_v2 B_lora2 B_tr2.0 F_sc0 B_tr2.1 B_atv0 B_tr2.2 B_atv1 B_sc0 B_atv2
    B_sc1 B_pt0 B_sc2 F_sc1 B_pv0 B_pt1 B_pt2 P_tok2 B_pv1 B_pv2 F_den0 F_den1 F_sc2 B_tr3.0 P_tr0.0
    F_sc3 B_tr3.1 F_av0 F_sc4 B_tr3.2 B_rk0 B_rk1 B_rk2 B_out0 B_out1 F_wo0 F_sc5 F_av1 B_out2
    P_tr0.1 F_wo1 F_av2 P_tr0.2 F_wo2
"""
ACT_BODY = """
    B_ct1.0 B_ct1.1 P_x0 B_ct1.2 F_k0 F_k1 B_ffn0 P_x1 B_ffn1 F_q0 B_z0 B_ffn2 B_z1 F_q1 F_spr0 P_x2
    B_z2 B_ap2.0 B_ap2.1 B_ct2.0 B_ct2.1 B_ap2.2 B_atv0 B_ct2.2 F_spr1 B_atv1 B_sc0 B_atv2 B_pt0
    B_sc1 B_sc2 B_pt1 B_pt2 B_ap3.0 P_ap0.0 B_ct3.0 B_ap3.1 B_ct3.1 B_ap3.2 B_ct3.2 P_ct0.0 B_rk0
    B_rk1 P_ap0.1 B_rk2 F_ap1.0 P_ct0.1 P_ap0.2 P_ct0.2 F_ap1.1 F_ap1.2
"""
DVE_BODY = """
    B_ffn0 B_h2a0 B_lmax0 F_k0 B_lsub0 B_ffn1 B_lmax1 B_lsub1 B_lrec0 B_ffn2 B_gate0 B_lmax2 B_lrec1
    B_h2a1 B_gate1 B_z0 B_z1 B_lsub2 F_k1 F_q0 B_lrec2 P_tok0 B_h2a2 B_gate2 P_st0.0 B_lora0 B_z2
    B_st2.0 B_lora1 B_mv2.0 B_ve2.0 F_v0 B_st2.1 F_cum0 B_mv2.1 B_ve2.1 F_v1 B_lora2 B_st2.2 B_mv2.2
    B_ve2.2 F_q1 P_tok1 F_sc0 B_sc0 F_cum1 P_mv0.0 B_smax0 B_nmax0 P_st0.1 B_sc1 B_prec0 P_mv0.1
    B_smax1 B_nmax1 B_sc2 B_smax2 F_v2 B_nmax2 F_sc1 B_prec1 B_pv0 P_ve0.0 B_st3.0 B_mv3.0 B_prec2
    P_ve0.1 B_ve3.0 P_tok2 P_st0.2 B_pv1 B_pv2 B_st3.1 B_st3.2 B_mv3.1 B_ve3.1 F_sc2 P_mv0.2 F_fl0
    F_fl1 B_mv3.2 B_ve3.2 B_xr0 F_sc3 B_xk0 B_xr1 B_xk1 B_xr2 B_xk2 F_rc0 F_rc1 P_lo0 F_av0 B_rkv0
    F_sc4 P_ve0.2 B_rkv1 F_wo0 F_st1.0 F_mv1.0 F_ve1.0 F_av1 F_sc5 B_rkv2 P_lo1 F_wo1 F_st1.1 F_av2
    F_mv1.1 F_ve1.1 P_lo2 F_wo2 F_st1.2 F_mv1.2 F_ve1.2
"""
POOL_BODY = """
    P_x0 P_x1 F_hbo0 F_hbo1 B_rs2.0 B_rs2.1 B_rs2.2 F_spread2 F_hbo2 P_x2 F_spread3 F_spread4 F_qk0
    F_qk1 F_spread5 P_rs0.0 B_rs3.0 B_rs3.1 B_xd0 B_rs3.2 P_rs0.1 B_xd1 B_xd2 B_out0 F_rs1.0 B_out1
    P_rs0.2 B_out2 F_hbb0 F_hbb1 F_rs1.1 F_rs1.2 F_hbb2
"""


def vit_tower_kernel(nc, a):
    out = a["out"].rearrange("b n e -> (b n) e")

    ctx = ExitStack()
    with ctx:
        def sb(name, shape, dt=F32):
            return ctx.enter_context(nc.sbuf_tensor(name, shape, dt))

        def sem(name):
            return ctx.enter_context(nc.semaphore(name))

        bank = [ctx.enter_context(nc.psum_tensor(f"bank{k}", [P, 512], F32)) for k in range(8)]

        names = ["L0_attn_Wk", "L0_attn_Wv", "L0_attn_Wq", "L0_attn_Wo",
                 "L1_attn_Qw", "L1_attn_Kw", "L1_attn_Vw", "L1_ffn_W_r", "L1_ffn_W_k", "L1_ffn_W_v"]
        wp_hi, wp_lo = sb("wp_hi", [P, KC, E], F32R), sb("wp_lo", [P, KC, E], F32R)
        WP_HALVES = [slice(0, KC // 2), slice(KC // 2, KC)]
        SPLIT = names[:3]
        w_hi = {n: sb(n + "_hi", [P, KT, E], F32R) for n in SPLIT}
        w_lo = {n: sb(n + "_lo", [P, KT, E], F32R) for n in SPLIT}
        wT = {n: sb(n + "_T", [P, KT, E]) for n in names[3:]}
        NCAT = E + NE + R
        wcat = sb("wcat", [P, KT, NCAT])
        G = sb("G", [P, KT, E])
        loraB = sb("loraB", [P, E])

        ident = sb("ident", [P, P])
        pos = sb("pos", [TMAX, E])
        bproj = sb("bproj", [TMAX, E])
        bv = sb("bv", [TMAX, E])
        bo = sb("bo", [TMAX, E])
        baseb = sb("baseb", [TMAX, E])
        routb = sb("routb", [TMAX, NE])
        bq = sb("bq", [P, KT])
        bk = sb("bk", [P, KT])
        bq1 = sb("bq1", [P, KT])
        bk1 = sb("bk1", [P, KT])
        nbq = sb("nbq", [P, KT])
        nbk = sb("nbk", [P, KT])
        mur = sb("mur", [P, KT])
        muk = sb("muk", [P, KT])
        mask01 = sb("mask01", [TMAX, TMAX])
        maskadd = sb("maskadd", [TMAX, TMAX])
        headmask = sb("headmask", [P, HPT])
        blockones = sb("blockones", [P, P])
        restart = sb("restart", [P, STOK])
        mhalf = sb("mhalf", [TMAX, 1])

        xT = sb("xT", [P, KC, STOK])
        x_hi, x_lo = sb("x_hi", [P, KC, STOK], F32R), sb("x_lo", [P, KC, STOK], F32R)
        xn0_hi, xn0_lo = sb("xn0_hi", [P, KT, STOK], F32R), sb("xn0_lo", [P, KT, STOK], F32R)
        hF = sb("hF", [TMAX, U, E])
        hbo = sb("hbo", [TMAX, U, E])
        kT = sb("kT", [P, KT, STOK])
        qT = sb("qT", [P, KT, STOK])
        qexp = sb("qexp", [P, KT, HPT, STOK])
        vpad = sb("vpad", [TMAX, U, NH // 2, 2, 2, DH])
        kcum = sb("kcum", [P, KT, STOK])
        kmin = kcum
        qk = sb("qk", [P, KT, STOK])
        qmin = qk
        rden = sb("rden", [P, KT, STOK])
        S = sb("S", [P, U, NH, TMAX])
        staged = S[:, :, :, :].rearrange("p u h t -> p (u h t)")
        wp_raw = staged[:, 0:KC * E].rearrange("p (c e) -> p c e", c=KC)
        w_raw = {n: staged[:, (KC + KT * j) * E:(KC + KT * (j + 1)) * E].rearrange("p (k e) -> p k e", k=KT)
                 for j, n in enumerate(SPLIT)}
        attnT = sb("attnT", [P, U, KT, TMAX])
        hB = sb("hB", [TMAX, U, E])
        hbb = sb("hbb", [TMAX, U, E])
        logit = sb("logit", [TMAX, U, NE])
        lmax = sb("lmax", [TMAX, U])
        lsub = sb("lsub", [TMAX, U, NE])
        lexp = sb("lexp", [TMAX, U, NE])
        lsum = sb("lsum", [TMAX, U])
        lrec = sb("lrec", [TMAX, U])
        gate = sb("gate", [TMAX, U, NE], BF16)
        mid = sb("mid", [TMAX, U, R])
        z = sb("z", [TMAX, U, P])
        zT = sb("zT", [P, U, TMAX])
        at = sb("at", [P, U, KT, TMAX])
        v1 = sb("v1", [TMAX, U, E])
        sm = sb("sm", [TMAX, U, TMAX])
        smax = sb("smax", [TMAX, U])
        nmax = sb("nmax", [TMAX, U])
        prob = sb("prob", [TMAX, U, TMAX])
        psm = sb("psm", [TMAX, U])
        prec = sb("prec", [TMAX, U])
        probT = sb("probT", [TMAX, U, TMAX])
        xs = sb("xs", [P, U, KT, 3, NTOK + 1])
        xd = sb("xd", [P, U, KT, TMAX])
        xr = sb("xr", [P, U, KT, TMAX])
        xk = sb("xk", [P, U, KT, TMAX])
        rt = sb("rt", [TMAX, U, E])
        rkv = sb("rkv", [TMAX, U, E])
        kact = sb("kact", [P, U, KT, TMAX])
        o_sb = sb("o_sb", [TMAX, U, E])

        xn_back = sb("xn_back", [TMAX, U, E])
        xnT_back = sb("xnT_back", [P, KT, STOK])

        class LN:
            def __init__(self, n):
                self.st = sb(f"ln{n}_st", [TMAX, U, 6])
                self.mv = sb(f"ln{n}_mv", [TMAX, U, 2])
                self.ve = sb(f"ln{n}_ve", [TMAX, U])
                self.nm = sb(f"ln{n}_nm", [TMAX, U])
                self.nb = sb(f"ln{n}_nb", [TMAX, U])
                self.rs = sb(f"ln{n}_rs", [TMAX, U])
                self.xn = xn_back if n else sb("xn_front", [TMAX, U, E])
                self.xnT = xnT_back if n else None
                self.stats_done = sem(f"ln{n}_stats_done")
                self.var_done = sem(f"ln{n}_var_done")
                self.pre_done = sem(f"ln{n}_pre_done")
                self.rstd_done = sem(f"ln{n}_rstd_done")
                self.xn_done = sem(f"ln{n}_xn_done")
                self.turned = sem(f"ln{n}_turned")
                self.xnT_ready = sem(f"ln{n}_xnT_ready")

        ln = [LN(n) for n in range(4)]

        s = {n: sem(n) for n in [
            "wp_hi_ready", "wp_lo_ready", "w_hi_ready", "w_lo_ready", "cat_loaded", "lora_loaded", "pos_loaded", "bproj_loaded", "rows_loaded", "vecs_loaded",
            "const_step", "ident_ready", "masks_ready", "zeros_ready", "pos_ready", "bias1_ready",
            "g_mm", "g_ready", "wv_halved",
            "x_hi_ready", "x_lo_ready", "xn0_lo_ready", "tok_mm", "hF_ready", "k_mm", "k_min", "k_exp", "kT_ready",
            "q_mm", "q_min", "q_exp", "qT_ready", "v_mm", "vpad_ready", "qexp_ready", "qexp_pool", "kcum_ready",
            "qk_ready", "den_mm", "den_floor", "rden_ready", "s_mm", "s_masked", "av_mm", "attnT_ready",
            "wo_mm", "hbo_ready", "h1_ready",
            "ffn_mm", "logit_ready", "lmax_ready", "lsub_ready", "lexp_ready", "lrec_ready", "gate_ready",
            "mid_ready", "z_ready", "hbb_ready", "h2a_ready", "z_turned", "zT_ready", "lora_mm", "h2_ready",
            "atv_mm", "at_ready", "v1_ready", "sc_mm", "sm_ready", "smax_ready", "nmax_ready", "prob_ready",
            "prob_turned", "probT_ready", "pv_mm", "prec_ready", "h3_ready", "xd_ready", "xr_ready",
            "xk_ready", "rk_mm", "rt_ready", "krelu_ready", "kact_ready", "kv_mm", "rkv_ready", "out_ready",
        ]}
        w_loaded = {n: sem(n + "_loaded") for n in names}
        wp_loaded = [sem(f"wp_loaded{j}") for j in range(len(WP_HALVES))]
        x_loaded = [sem(f"x_loaded{u}") for u in range(U)]
        out_stored = [sem(f"out_stored{u}") for u in range(U)]

        TOK_BANK, K_BANK, Q_BANK, V_BANK, S_BANK, AV_BANK, WO_BANK = 0, [1, 2], [3, 4], [1, 2, 3], [1, 2], 3, 4
        DEN_BANK = [4, 3]

        def tr(n, u):
            b = TOK_BANK if n == 0 else FB + u
            return bank[b][:, 0:KT * T[u]].rearrange("p (k t) -> p k t", k=KT)

        block = ctx.enter_context(nc.Block())

        AHEAD = {"P": 1, "F": 0, "B": -1}

        def run(eng, steps, body, first={}):
            body = body.split()

            def turn(i, kinds):
                for name in body:
                    if name[0] in kinds:
                        j = i + AHEAD[name[0]]
                        if isinstance(j, int) and j == 0 and name in first:
                            first[name]()
                        steps[name[:-1].rstrip(".")](j, int(name[-1]))

            turn(-1, "P")
            turn(0, "PF")
            with eng.Fori(1, STEPS - 1) as i:
                turn(i, "PFB")
            turn(STEPS - 1, "FB")
            turn(STEPS, "B")

        @block.sync
        def _(sp):
            def load_x(i, u):
                sp.dma_start(xT[:, :, OFF[u]:OFF[u] + T[u]],
                             a["x"][bass.ds(i * P, P), :, OFF[u]:OFF[u] + T[u]]).then_inc(x_loaded[u], 16)

            def load_w(n, dst, signal):
                sp.dma_start(dst, a[n].rearrange("(t p) n -> p t n", p=P)).then_inc(signal, 16)

            def row(dst, n, signal="rows_loaded"):
                v = a[n].rearrange("(o n) -> o n", o=1)
                sp.dma_start(dst, v.to_broadcast([TMAX, v.shape[1]])).then_inc(s[signal], 16)

            for j, h in enumerate(WP_HALVES):
                sp.dma_start(wp_raw[:, h, :], a["L0_tok_W_proj"].rearrange("(t p) n -> p t n", p=P)[:, h, :]
                             ).then_inc(wp_loaded[j], 16)
            for u in range(U):
                load_x(0, u)
            for k in range(3):
                sp.dma_start(pos[k * NTOK:(k + 1) * NTOK, :], a["L0_tok_pos_emb"]).then_inc(s["pos_loaded"], 16)
            row(bproj[:, :], "L0_tok_b_proj", "bproj_loaded")
            for n in SPLIT:
                load_w(n, w_raw[n], w_loaded[n])
            with nc.allow_non_contiguous_dma("per-feature vectors, four bytes a partition"):
                for dst, n in ((bq, "L0_attn_bq"), (bk, "L0_attn_bk"), (mur, "L1_ffn_mu_r"), (muk, "L1_ffn_mu_k")):
                    sp.dma_start(dst[:, :], a[n].rearrange("(t p) -> p t", p=P)).then_inc(s["vecs_loaded"], 16)
            row(bv[:, :], "L0_attn_bv")
            row(bo[:, :], "L0_attn_bo")
            row(baseb[:, :], "L0_ffn_base_b")
            row(routb[:, :], "L0_ffn_router_b")
            load_w(names[3], wT[names[3]][:, :, :], w_loaded[names[3]])
            load_w("L0_ffn_cat", wcat[:, :, :], s["cat_loaded"])
            sp.dma_start(loraB[0:NE * R, :], a["L0_ffn_lora_B"]).then_inc(s["lora_loaded"], 16)
            for n in names[4:]:
                load_w(n, wT[n][:, :, :], w_loaded[n])

            def store(i):
                for u in range(U):
                    sp.wait_ge(s["out_ready"], U * i + u + 1)
                    sp.dma_start(out[bass.ds(i * STOK + OFF[u], T[u]), :],
                                 o_sb[0:T[u], u, :]).then_inc(out_stored[u], 16)

            def fetch(i):
                for u in range(U):
                    sp.wait_ge(s["x_lo_ready"], U * (i - 1) + u + 1)
                    load_x(i, u)

            fetch(1)
            with sp.Fori(1, STEPS - 1) as i:
                fetch(i + 1)
                store(i - 1)
            store(STEPS - 2)
            store(STEPS - 1)
            for u in range(U):
                sp.wait_ge(out_stored[u], 16 * STEPS + 1)

        @block.gpsimd
        def _(pool):
            nc.gpsimd.memset(ident[:, :], 0.0).then_inc(s["const_step"], 1)
            pool.wait_ge(s["const_step"], 1)
            nc.gpsimd.affine_select(ident[:, :], ident[:, :], pattern=[[-1, P]], compare_op=ALU.not_equal,
                                    fill=1.0, base=0, channel_multiplier=1).then_inc(s["ident_ready"], 1)
            c = [1]

            def link(ins):
                ins.then_inc(s["const_step"], 1)
                c[0] += 1
                pool.wait_ge(s["const_step"], c[0])

            nc.gpsimd.memset(mhalf[:, :], -0.5)
            nc.gpsimd.memset(mask01[:, :], 1.0)
            nc.gpsimd.memset(maskadd[:, :], 0.0)
            nc.gpsimd.memset(headmask[:, :], 1.0)
            link(nc.gpsimd.memset(blockones[:, :], 1.0))
            m01 = mask01[:, :].rearrange("p (b t) -> p b t", b=3)
            mad = maskadd[:, :].rearrange("p (b t) -> p b t", b=3)
            bl = blockones[:, :].rearrange("p (h d) -> p h d", h=HPT)
            hd = headmask[:, :]
            nc.gpsimd.affine_select(m01, m01, pattern=[[NTOK, 3], [1, NTOK]], compare_op=ALU.is_ge, fill=0.0,
                                    base=0, channel_multiplier=-1)
            nc.gpsimd.affine_select(mad, mad, pattern=[[-NTOK, 3], [-1, NTOK]], compare_op=ALU.is_ge, fill=NEG,
                                    base=0, channel_multiplier=1)
            nc.gpsimd.affine_select(hd, hd, pattern=[[-DH, HPT]], compare_op=ALU.is_ge, fill=0.0,
                                    base=0, channel_multiplier=1)
            link(nc.gpsimd.affine_select(bl, bl, pattern=[[-DH, HPT], [0, DH]], compare_op=ALU.is_ge, fill=0.0,
                                         base=0, channel_multiplier=1))
            nc.gpsimd.affine_select(m01, m01, pattern=[[-NTOK, 3], [0, NTOK]], compare_op=ALU.is_ge, fill=0.0,
                                    base=0, channel_multiplier=1)
            nc.gpsimd.affine_select(mad, mad, pattern=[[NTOK, 3], [0, NTOK]], compare_op=ALU.is_ge, fill=NEG,
                                    base=NTOK - 1, channel_multiplier=-1)
            nc.gpsimd.affine_select(hd, hd, pattern=[[DH, HPT]], compare_op=ALU.is_ge, fill=0.0,
                                    base=DH - 1, channel_multiplier=-1)
            nc.gpsimd.affine_select(bl, bl, pattern=[[DH, HPT], [0, DH]], compare_op=ALU.is_ge, fill=0.0,
                                    base=DH - 1, channel_multiplier=-1).then_inc(s["masks_ready"], 1)
            pool.wait_ge(s["pos_loaded"], 48)
            pool.wait_ge(s["bproj_loaded"], 16)
            nc.gpsimd.tensor_tensor(pos[:, :], pos[:, :], bproj[:, :], ALU.add).then_inc(s["pos_ready"], 1)

            def rstd(n, i, u):
                L, t, c = ln[n], T[u], U * i + u + 1
                pool.wait_ge(L.pre_done, c)
                nc.gpsimd.tensor_tensor(L.rs[0:t, u:u + 1], L.ve[0:t, u:u + 1], mhalf[0:t, :],
                                        ALU.pow).then_inc(L.rstd_done, 1)
                pool.wait_ge(L.rstd_done, 2 * U * i + 2 * u + 1)
                nc.gpsimd.tensor_tensor(L.nb[0:t, u:u + 1], L.nm[0:t, u:u + 1], L.rs[0:t, u:u + 1],
                                        ALU.mult).then_inc(L.rstd_done, 1)

            def f_x(i, u):
                if isinstance(i, int) and i == 0:
                    return
                o, t = OFF[u], T[u]
                pool.wait_ge(s["x_hi_ready"], U * i + u + 1)
                nc.gpsimd.tensor_tensor(x_lo[:, :, o:o + t], xT[:, :, o:o + t], x_hi[:, :, o:o + t].bitcast(F32),
                                        ALU.subtract).then_inc(s["x_lo_ready"], 1)

            def f_hbo(i, u):
                pool.wait_ge(s["hF_ready"], U * i + u + 1)
                if not (isinstance(i, int) and i == 0):
                    pool.wait_ge(s["h1_ready"], U * (i - 1) + u + 1)
                if isinstance(i, int) and i == 0 and u == 0:
                    pool.wait_ge(s["rows_loaded"], 16 * 4)
                nc.gpsimd.tensor_tensor(hbo[0:T[u], u, :], hF[0:T[u], u, :], bo[0:T[u], :],
                                        ALU.add).then_inc(s["hbo_ready"], 1)

            def f_hbb(i, u):
                pool.wait_ge(s["h1_ready"], U * i + u + 1)
                nc.gpsimd.tensor_tensor(hbb[0:T[u], u, :], hB[0:T[u], u, :], baseb[0:T[u], :],
                                        ALU.add).then_inc(s["hbb_ready"], 1)

            def b_xd(i, u):
                n = IMGS[u]
                pool.wait_ge(ln[3].xnT_ready, KT * (U * i + u + 1))
                for k in range(KT):
                    ins = nc.gpsimd.tensor_tensor(xd[:, u, k, 0:T[u]].rearrange("p (b t) -> p b t", b=n),
                                                  xs[:, u, k, 0:n, 1:NTOK + 1], xs[:, u, k, 0:n, 0:NTOK],
                                                  ALU.subtract)
                ins.then_inc(s["xd_ready"], 1)

            def spread(i, j):
                u, ft = j // KT, j % KT
                o, t = OFF[u], T[u]
                pool.wait_ge(s["qT_ready"], KT * i + ft + 1)
                nc.gpsimd.tensor_tensor(
                    qexp[:, ft, :, o:o + t], qT[:, ft:ft + 1, o:o + t].to_broadcast([P, HPT, t]),
                    headmask[:, :].rearrange("p (h o) -> p h o", o=1).to_broadcast([P, HPT, t]),
                    ALU.mult).then_inc(s["qexp_pool"], 1)

            def f_qk(i, ft):
                pool.wait_ge(s["qT_ready"], KT * i + ft + 1)
                pool.wait_ge(s["kcum_ready"], KT * i + ft + 1)
                nc.gpsimd.tensor_tensor(qk[:, ft, :], qT[:, ft, :], kcum[:, ft, :],
                                        ALU.mult).then_inc(s["qk_ready"], 1)

            def b_out(i, u):
                t = T[u]
                pool.wait_ge(s["rkv_ready"], U * i + u + 1)
                pool.wait_ge(out_stored[u], 16 * i + 1)
                nc.gpsimd.tensor_tensor(o_sb[0:t, u, :], rkv[0:t, u, :], hB[0:t, u, :],
                                        ALU.add).then_inc(s["out_ready"], 1)

            run(pool, {"F_qk": f_qk, "B_out": b_out, "P_x": f_x, "F_hbo": f_hbo, "F_hbb": f_hbb, "F_spread": spread, "B_xd": b_xd,
                       "P_rs0": lambda i, u: rstd(0, i, u), "F_rs1": lambda i, u: rstd(1, i, u),
                       "B_rs2": lambda i, u: rstd(2, i, u), "B_rs3": lambda i, u: rstd(3, i, u)},
                POOL_BODY)

        @block.tensor
        def _(pe):
            def w_g():
                qw, kw = wT["L1_attn_Qw"], wT["L1_attn_Kw"]
                pe.wait_ge(w_loaded["L1_attn_Qw"], 16)
                pe.wait_ge(w_loaded["L1_attn_Kw"], 16)
                for ft in range(KT):
                    for dt in range(KT):
                        ins = nc.tensor.matmul(bank[7][:, ft * E:(ft + 1) * E], qw[:, dt, ft * P:(ft + 1) * P],
                                               kw[:, dt, :], start=(dt == 0), stop=(dt == KT - 1))
                ins.then_inc(s["g_mm"], 1)
                for n in names[6:-1]:
                    pe.wait_ge(w_loaded[n], 16)
                pe.wait_ge(s["cat_loaded"], 16)
                pe.wait_ge(s["lora_loaded"], 16)
                pe.wait_ge(s["zeros_ready"], 1)
                pe.wait_ge(s["g_ready"], 1)
                pe.wait_ge(s["wv_halved"], 1)

            def product3(out_ap, pairs):
                terms = [(a[x], b[y]) for a, b in pairs for x, y in ((0, 0), (0, 1), (1, 0))]
                for n, (lhs, rhs) in enumerate(terms):
                    ins = nc.tensor.matmul(out_ap, lhs, rhs, start=(n == 0), stop=(n == len(terms) - 1))
                return ins

            def f_tok(i, u):
                o, t = OFF[u], T[u]
                if isinstance(i, int) and i == 0:
                    pe.wait_ge(s["wp_hi_ready"], len(WP_HALVES))
                    pe.wait_ge(s["wp_lo_ready"], len(WP_HALVES))
                if u:
                    pe.wait_ge(s["hF_ready"], U * i + u)
                elif not isinstance(i, int) or i > 0:
                    pe.wait_ge(s["xn0_lo_ready"], U * i)
                pe.wait_ge(s["x_hi_ready"], U * i + u + 1)
                pe.wait_ge(s["x_lo_ready"], U * i + u + 1)
                product3(bank[TOK_BANK][0:t, 0:E],
                         [((x_hi[:, c, o:o + t], x_lo[:, c, o:o + t]), (wp_hi[:, c, :], wp_lo[:, c, :]))
                          for c in range(KC)]).then_inc(s["tok_mm"], 1)

            def turn_ln(n):
                def step(i, u):
                    pe.wait_ge(ln[n].xn_done, U * i + u + 1)
                    if n == 0:
                        if u:
                            pe.wait_ge(s["xn0_lo_ready"], U * i + u)
                        else:
                            pe.wait_ge(s["hF_ready"], U * i + U)
                    for k in range(KT):
                        ins = nc.tensor.transpose(tr(n, u)[:, k, :], ln[n].xn[0:T[u], u, k * P:(k + 1) * P],
                                                  ident[0:T[u], 0:T[u]])
                    ins.then_inc(ln[n].turned, 1)
                return step

            def wide(w, ft, b, done):
                product3(bank[b][:, 0:STOK],
                         [((w_hi[w][:, k, ft * P:(ft + 1) * P], w_lo[w][:, k, ft * P:(ft + 1) * P]),
                           (xn0_hi[:, k, :], xn0_lo[:, k, :])) for k in range(KT)]).then_inc(s[done], 1)

            def f_k(i, ft):
                if ft == 0:
                    pe.wait_ge(ln[0].xnT_ready, U * i + U)
                    pe.wait_ge(s["xn0_lo_ready"], U * i + U)
                    if isinstance(i, int) and i == 0:
                        pe.wait_ge(s["w_hi_ready"], len(SPLIT))
                        pe.wait_ge(s["w_lo_ready"], len(SPLIT))
                wide("L0_attn_Wk", ft, K_BANK[ft], "k_mm")

            def f_v(i, u):
                o, t, w = OFF[u], T[u], "L0_attn_Wv"
                pe.wait_ge(s["kT_ready" if u < KT else "qT_ready"], KT * i + (u % KT) + 1)
                product3(bank[V_BANK[u]][0:t, 0:E],
                         [((xn0_hi[:, k, o:o + t], xn0_lo[:, k, o:o + t]), (w_hi[w][:, k, :], w_lo[w][:, k, :]))
                          for k in range(KT)]).then_inc(s["v_mm"], 1)

            def f_q(i, ft):
                if ft == 1 and not (isinstance(i, int) and i == 0):
                    pe.wait_ge(s["h1_ready"], U * i)
                wide("L0_attn_Wq", ft, Q_BANK[ft], "q_mm")

            def f_sc(i, ju):
                u, ft = ju // KT, ju % KT
                if u == 0:
                    pe.wait_ge(s["qexp_ready"], KT * i + ft + 1)
                else:
                    pe.wait_ge(s["qexp_pool"], KT * (U - 1) * i + ju - KT + 1)
                for half in range(2):
                    j = 2 * ju + half
                    if j == 0:
                        pe.wait_ge(s["kT_ready"], KT * i + KT)
                    if j < 2:
                        pe.wait_ge(s["vpad_ready"], U * i + j + 1)
                    else:
                        pe.wait_ge(s["s_masked"], 12 * i + j - 1)
                    nc.tensor.matmul(
                        bank[S_BANK[j % 2]][0:T[u], 0:4 * T[u]].rearrange("p (h t) -> p h t", h=4),
                        kT[:, ft, OFF[u]:OFF[u] + T[u]],
                        qexp[:, ft, 4 * half:4 * half + 4, OFF[u]:OFF[u] + T[u]],
                        start=True, stop=True).then_inc(s["s_mm"], 1)

            def f_den(i, ft):
                pe.wait_ge(s["qk_ready"], KT * i + ft + 1)
                if ft == 1:
                    pe.wait_ge(s["vpad_ready"], U * i + U)
                nc.tensor.matmul(bank[DEN_BANK[ft]][:, 0:STOK], blockones[:, :], qk[:, ft, :],
                                 start=True, stop=True).then_inc(s["den_mm"], 1)

            def f_av(i, u):
                pe.wait_ge(s["s_masked"], 12 * i + 4 * u + 4)
                if u == 0:
                    pe.wait_ge(s["den_floor"], KT * i + KT)
                else:
                    pe.wait_ge(s["attnT_ready"], U * i + u)
                for ft in range(KT):
                    for e in range(2):
                        for r in range(4):
                            pair = 4 * ft + r
                            ins = nc.tensor.matmul(
                                bank[AV_BANK][32 * r:32 * r + 32, ft * T[u]:(ft + 1) * T[u]],
                                vpad[0:T[u], u, pair, e, :, :].rearrange("p a d -> p (a d)"),
                                S[0:T[u], u, 2 * pair + e, 0:T[u]], start=(e == 0), stop=(e == 1),
                                tile_position=(0, 32 * r))
                ins.then_inc(s["av_mm"], 1)

            def project(b, t, lhs, w, done):
                for k in range(KT):
                    ins = nc.tensor.matmul(bank[b][0:t, 0:w.shape[2]], lhs(k), w[:, k, :],
                                           start=(k == 0), stop=(k == KT - 1))
                ins.then_inc(s[done], 1)

            def f_wo(i, u):
                pe.wait_ge(s["attnT_ready"], U * i + u + 1)
                if u == 0:
                    if isinstance(i, int) and i == 0:
                        pe.wait_ge(w_loaded["L0_attn_Wo"], 16)
                else:
                    pe.wait_ge(s["h1_ready"], U * i + u)
                project(WO_BANK, T[u], lambda k: attnT[:, u, k, 0:T[u]], wT["L0_attn_Wo"], "wo_mm")

            def b_ffn(i, u):
                pe.wait_ge(ln[1].xnT_ready, U * i + u + 1)
                project(FB + u, T[u], lambda k: ln[1].xnT[:, k, OFF[u]:OFF[u] + T[u]], wcat, "ffn_mm")

            def b_z(i, u):
                pe.wait_ge(s["z_ready"], U * i + u + 1)
                pe.wait_ge(s["h2a_ready"], U * i + u + 1)
                nc.tensor.transpose(bank[FB + u][:, 0:T[u]], z[0:T[u], u, :],
                                    ident[0:T[u], 0:T[u]]).then_inc(s["z_turned"], 1)

            def b_lora(i, u):
                pe.wait_ge(s["zT_ready"], U * i + u + 1)
                nc.tensor.matmul(bank[FB + u][0:T[u], 0:E], zT[:, u, 0:T[u]], loraB[:, :],
                                 start=True, stop=True).then_inc(s["lora_mm"], 1)

            def b_atv(i, u):
                pe.wait_ge(ln[2].xnT_ready, U * i + u + 1)
                for ft in range(KT):
                    for k in range(KT):
                        nc.tensor.matmul(bank[FB + u][:, ft * T[u]:(ft + 1) * T[u]],
                                         G[:, k, ft * P:(ft + 1) * P], ln[2].xnT[:, k, OFF[u]:OFF[u] + T[u]],
                                         start=(k == 0), stop=(k == KT - 1))
                for k in range(KT):
                    ins = nc.tensor.matmul(bank[FB + u][0:T[u], E:2 * E], ln[2].xnT[:, k, OFF[u]:OFF[u] + T[u]],
                                           wT["L1_attn_Vw"][:, k, :], start=(k == 0), stop=(k == KT - 1))
                ins.then_inc(s["atv_mm"], 1)

            def b_sc(i, u):
                pe.wait_ge(s["at_ready"], U * i + u + 1)
                pe.wait_ge(s["v1_ready"], U * i + u + 1)
                for k in range(KT):
                    ins = nc.tensor.matmul(bank[FB + u][0:T[u], 0:T[u]], at[:, u, k, 0:T[u]],
                                           ln[2].xnT[:, k, OFF[u]:OFF[u] + T[u]],
                                           start=(k == 0), stop=(k == KT - 1))
                ins.then_inc(s["sc_mm"], 1)

            def b_pt(i, u):
                pe.wait_ge(s["prob_ready"], U * i + u + 1)
                nc.tensor.transpose(bank[FB + u][0:T[u], 0:T[u]], prob[0:T[u], u, 0:T[u]],
                                    ident[0:T[u], 0:T[u]]).then_inc(s["prob_turned"], 1)

            def b_pv(i, u):
                pe.wait_ge(s["probT_ready"], U * i + u + 1)
                nc.tensor.matmul(bank[FB + u][0:T[u], 0:E], probT[0:T[u], u, 0:T[u]], v1[0:T[u], u, :],
                                 start=True, stop=True).then_inc(s["pv_mm"], 1)

            def b_rk(i, u):
                pe.wait_ge(s["xr_ready"], U * i + u + 1)
                for k in range(KT):
                    nc.tensor.matmul(bank[FB + u][0:T[u], 0:E], xr[:, u, k, 0:T[u]],
                                     wT["L1_ffn_W_r"][:, k, :], start=(k == 0), stop=(k == KT - 1))
                pe.wait_ge(s["xk_ready"], U * i + u + 1)
                for ft in range(KT):
                    for k in range(KT):
                        ins = nc.tensor.matmul(bank[FB + u][:, E + ft * T[u]:E + (ft + 1) * T[u]],
                                               wT["L1_ffn_W_k"][:, k, ft * P:(ft + 1) * P],
                                               xk[:, u, k, 0:T[u]], start=(k == 0), stop=(k == KT - 1))
                ins.then_inc(s["rk_mm"], 1)

            def b_out(i, u):
                pe.wait_ge(s["kact_ready"], U * i + u + 1)
                pe.wait_ge(s["rt_ready"], U * i + u + 1)
                project(FB + u, T[u], lambda k: kact[:, u, k, 0:T[u]], wT["L1_ffn_W_v"], "kv_mm")

            pe.wait_ge(s["ident_ready"], 1)
            run(pe, {"P_tok": f_tok, "P_tr0": turn_ln(0), "F_k": f_k, "F_v": f_v, "F_q": f_q,
                     "F_sc": f_sc, "F_den": f_den, "F_av": f_av, "F_wo": f_wo,
                     "B_tr1": turn_ln(1), "B_ffn": b_ffn, "B_z": b_z, "B_lora": b_lora, "B_tr2": turn_ln(2),
                     "B_atv": b_atv, "B_sc": b_sc, "B_pt": b_pt, "B_pv": b_pv, "B_tr3": turn_ln(3),
                     "B_rk": b_rk, "B_out": b_out}, PE_BODY, {"F_av0": w_g})

        @block.scalar
        def _(act):
            def copy(dst, src):
                return nc.scalar.activation(dst, src, ACT.Copy)

            def w_g():
                act.wait_ge(s["g_mm"], 1)
                copy(G[:, :, :], bank[7][:, :].rearrange("p (k e) -> p k e", k=KT)).then_inc(s["g_ready"], 1)
                wv = wT["L1_ffn_W_v"]
                act.wait_ge(w_loaded["L1_ffn_W_v"], 16)
                nc.scalar.activation(wv[:, :, :], wv[:, :, :], ACT.Copy, scale=0.5).then_inc(s["wv_halved"], 1)

            def f_x(i, u):
                o, t = OFF[u], T[u]
                act.wait_ge(x_loaded[u], 16 * i + 16)
                copy(x_hi[:, :, o:o + t], xT[:, :, o:o + t]).then_inc(s["x_hi_ready"], 1)

            def f_x_later(i, u):
                if not (isinstance(i, int) and i == 0):
                    f_x(i, u)

            def apply_ln(n, h):
                def step(i, u):
                    L, t = ln[n], T[u]
                    act.wait_ge(L.rstd_done, 2 * (U * i + u + 1))
                    nc.scalar.activation(L.xn[0:t, u, :], h[0:t, u, :], ACT.Identity, bias=L.nb[0:t, u:u + 1],
                                         scale=L.rs[0:t, u:u + 1]).then_inc(L.xn_done, 1)
                return step

            def take_turned(n):
                def step(i, u):
                    act.wait_ge(ln[n].turned, U * i + u + 1)
                    if n == 0:
                        if not (isinstance(i, int) and i == 0):
                            act.wait_ge(s["v_mm"], U * i)
                        copy(xn0_hi[:, :, OFF[u]:OFF[u] + T[u]], tr(n, u)).then_inc(ln[n].xnT_ready, 1)
                    elif n == 3:
                        for k in range(KT):
                            copy(xs[:, u, k, 0:IMGS[u], 1:NTOK + 1],
                                 tr(n, u)[:, k, :].rearrange("p (b t) -> p b t", b=IMGS[u])
                                 ).then_inc(ln[n].xnT_ready, 1)
                    else:
                        copy(ln[n].xnT[:, :, OFF[u]:OFF[u] + T[u]], tr(n, u)).then_inc(ln[n].xnT_ready, 1)
                return step

            def feature_exp(name, banks, nbias, dst):
                def step(i, ft):
                    act.wait_ge(s[f"{name}_mm"], KT * i + ft + 1)
                    nc.scalar.activation(dst[:, ft, :], bank[banks[ft]][:, 0:STOK], ACT.Relu,
                                         bias=nbias[:, ft:ft + 1], scale=-1.0).then_inc(s[f"{name}_min"], 1)
                    act.wait_ge(s[f"{name}_min"], KT * i + ft + 1)
                    nc.scalar.activation(dst[:, ft, :], dst[:, ft, :], ACT.Exp, scale=-1.0
                                         ).then_inc(s[f"{name}_exp"], 1)
                return step

            def f_spread(i, ft):
                t = T[0]
                act.wait_ge(s["qT_ready"], KT * i + ft + 1)
                for h in range(HPT):
                    ins = nc.scalar.activation(qexp[:, ft, h, 0:t], qT[:, ft, 0:t], ACT.Copy,
                                               scale=headmask[:, h:h + 1])
                ins.then_inc(s["qexp_ready"], 1)

            def b_ffn(i, u):
                t = T[u]
                act.wait_ge(s["lsub_ready"], U * i + u + 1)
                nc.scalar.activation(lexp[0:t, u, :], lsub[0:t, u, :], ACT.Exp,
                                     accum_out=lsum[0:t, u:u + 1]).then_inc(s["lexp_ready"], 1)

            def b_z(i, u):
                act.wait_ge(s["z_turned"], U * i + u + 1)
                copy(zT[:, u, 0:T[u]], bank[FB + u][:, 0:T[u]]).then_inc(s["zT_ready"], 1)

            def b_atv(i, u):
                t = T[u]
                act.wait_ge(s["atv_mm"], U * i + u + 1)
                copy(at[:, u, :, 0:t], bank[FB + u][:, 0:KT * t].rearrange("p (k t) -> p k t", k=KT)
                     ).then_inc(s["at_ready"], 1)
                copy(v1[0:t, u, :], bank[FB + u][0:t, E:2 * E]).then_inc(s["v1_ready"], 1)

            def b_sc(i, u):
                t = T[u]
                act.wait_ge(s["nmax_ready"], U * i + u + 1)
                nc.scalar.activation(prob[0:t, u, 0:t], sm[0:t, u, 0:t], ACT.Exp, bias=nmax[0:t, u:u + 1],
                                     scale=float(E) ** -0.5, accum_out=psm[0:t, u:u + 1]
                                     ).then_inc(s["prob_ready"], 1)

            def b_pt(i, u):
                act.wait_ge(s["prob_turned"], U * i + u + 1)
                copy(probT[0:T[u], u, 0:T[u]], bank[FB + u][0:T[u], 0:T[u]]).then_inc(s["probT_ready"], 1)

            def b_rk(i, u):
                t = T[u]
                act.wait_ge(s["rk_mm"], U * i + u + 1)
                nc.scalar.activation(kact[:, u, :, 0:t],
                                     bank[FB + u][:, E:E + KT * t].rearrange("p (k t) -> p k t", k=KT),
                                     ACT.Relu).then_inc(s["krelu_ready"], 1)
                nc.scalar.activation(rt[0:t, u, :], bank[FB + u][0:t, 0:E], ACT.Tanh, scale=0.5
                                     ).then_inc(s["rt_ready"], 1)
                act.wait_ge(s["krelu_ready"], U * i + u + 1)
                nc.scalar.activation(kact[:, u, :, 0:t], kact[:, u, :, 0:t], ACT.Square
                                     ).then_inc(s["kact_ready"], 1)

            for j, h in enumerate(WP_HALVES):
                act.wait_ge(wp_loaded[j], 16)
                copy(wp_hi[:, h, :], wp_raw[:, h, :]).then_inc(s["wp_hi_ready"], 1)
            for u in range(U):
                f_x(0, u)
            for n in SPLIT:
                act.wait_ge(w_loaded[n], 16)
                copy(w_hi[n][:, :, :], w_raw[n]).then_inc(s["w_hi_ready"], 1)
            run(act, {"P_x": f_x_later, "P_ap0": apply_ln(0, hF), "P_ct0": take_turned(0),
                      "F_k": feature_exp("k", K_BANK, nbk, kmin), "F_q": feature_exp("q", Q_BANK, nbq, qmin),
                      "F_spr": f_spread, "F_ap1": apply_ln(1, hB), "B_ct1": take_turned(1), "B_ffn": b_ffn, "B_z": b_z,
                      "B_ap2": apply_ln(2, hB), "B_ct2": take_turned(2),
                      "B_atv": b_atv, "B_sc": b_sc, "B_pt": b_pt, "B_ap3": apply_ln(3, hB),
                      "B_ct3": take_turned(3), "B_rk": b_rk}, ACT_BODY,
                {"F_k0": lambda: act.wait_ge(s["bias1_ready"], 1), "F_spr0": lambda: act.wait_ge(s["masks_ready"], 1),
                 "F_ap1.0": w_g})

        @block.vector
        def _(dve):
            nc.vector.memset(vpad[:, :, :, :, :, :], 0.0)
            nc.vector.memset(z[:, :, :], 0.0)
            for u in range(U):
                nc.vector.memset(o_sb[:, u, 0:1], 0.0).then_inc(out_stored[u], 1)
            nc.vector.memset(xs[:, :, :, :, 0:1], 0.0)
            nc.vector.memset(restart[:, :], 1.0)
            nc.vector.memset(loraB[NE * R:P, :], 0.0).then_inc(s["zeros_ready"], 1)
            dve.wait_ge(s["zeros_ready"], 1)
            rs_v = restart[:, :].rearrange("p (b t) -> p b t", b=STEP_IMGS)
            nc.vector.memset(rs_v[:, :, 0:1], 0.0).then_inc(s["zeros_ready"], 1)
            for j, h in enumerate(WP_HALVES):
                dve.wait_ge(s["wp_hi_ready"], j + 1)
                nc.vector.tensor_tensor(wp_lo[:, h, :], wp_raw[:, h, :], wp_hi[:, h, :].bitcast(F32),
                                        ALU.subtract).then_inc(s["wp_lo_ready"], 1)
            for u in range(U):
                o, t = OFF[u], T[u]
                dve.wait_ge(s["x_hi_ready"], u + 1)
                nc.vector.tensor_tensor(x_lo[:, :, o:o + t], xT[:, :, o:o + t], x_hi[:, :, o:o + t].bitcast(F32),
                                        ALU.subtract).then_inc(s["x_lo_ready"], 1)
            dve.wait_ge(s["pos_ready"], 1)

            def w_split():
                for j, n in enumerate(SPLIT):
                    dve.wait_ge(s["w_hi_ready"], j + 1)
                    nc.vector.tensor_tensor(w_lo[n][:, :, :], w_raw[n], w_hi[n][:, :, :].bitcast(F32),
                                            ALU.subtract).then_inc(s["w_lo_ready"], 1)
                dve.wait_ge(s["vecs_loaded"], 64)
                nc.vector.tensor_scalar(bk1[:, :], bk[:, :], 1.0, None, ALU.add)
                nc.vector.tensor_scalar(nbk[:, :], bk[:, :], -1.0, None, ALU.mult)
                nc.vector.tensor_scalar(nbq[:, :], bq[:, :], -1.0, None, ALU.mult)
                nc.vector.tensor_scalar(bq1[:, :], bq[:, :], 1.0, None, ALU.add).then_inc(s["bias1_ready"], 1)
                dve.wait_ge(s["bias1_ready"], 1)
                dve.wait_ge(s["zeros_ready"], 2)
                dve.wait_ge(s["rows_loaded"], 16 * 4)
                dve.wait_ge(s["masks_ready"], 1)

            def stats(n, h, h_ready):
                def step(i, u):
                    L, t = ln[n], T[u]
                    dve.wait_ge(h_ready, U * i + u + 1)
                    nc.vector.bn_stats(L.st[0:t, u, :], h[0:t, u, :]).then_inc(L.stats_done, 1)
                return step

            def mean_var(n):
                def step(i, u):
                    L, t = ln[n], T[u]
                    dve.wait_ge(s["pos_ready"], 1)
                    dve.wait_ge(L.stats_done, U * i + u + 1)
                    nc.vector.bn_aggr(L.mv[0:t, u, :], L.st[0:t, u, :]).then_inc(L.var_done, 1)
                return step

            def var_eps(n):
                def step(i, u):
                    L, t = ln[n], T[u]
                    dve.wait_ge(L.var_done, U * i + u + 1)
                    nc.vector.tensor_scalar(L.ve[0:t, u:u + 1], L.mv[0:t, u, 1:2], LN_EPS, None, ALU.add)
                    nc.vector.tensor_scalar(L.nm[0:t, u:u + 1], L.mv[0:t, u, 0:1], -1.0, None,
                                            ALU.mult).then_inc(L.pre_done, 1)
                return step

            def f_tok(i, u):
                t = T[u]
                dve.wait_ge(s["tok_mm"], U * i + u + 1)
                if not (isinstance(i, int) and i == 0):
                    dve.wait_ge(s["hbo_ready"], U * (i - 1) + u + 1)
                nc.vector.tensor_tensor(hF[0:t, u, :], bank[TOK_BANK][0:t, 0:E], pos[0:t, :],
                                        ALU.add).then_inc(s["hF_ready"], 1)

            def f_tr(i, u):
                o, t = OFF[u], T[u]
                dve.wait_ge(ln[0].xnT_ready, U * i + u + 1)
                nc.vector.tensor_tensor(xn0_lo[:, :, o:o + t], tr(0, u), xn0_hi[:, :, o:o + t].bitcast(F32),
                                        ALU.subtract).then_inc(s["xn0_lo_ready"], 1)

            def feature(name, banks, bias1, src, dst):
                def step(i, ft):
                    dve.wait_ge(s[f"{name}_exp"], KT * i + ft + 1)
                    nc.vector.scalar_tensor_tensor(out=dst[:, ft, :], in0=bank[banks[ft]][:, 0:STOK],
                                                   scalar=bias1[:, ft:ft + 1], in1=src[:, ft, :],
                                                   op0=ALU.add, op1=ALU.max).then_inc(s[f"{name}T_ready"], 1)
                return step

            feature_k = feature("k", K_BANK, bk1, kmin, kT)
            feature_q = feature("q", Q_BANK, bq1, qmin, qT)

            def f_v(i, u):
                t, b = T[u], V_BANK[u]
                dve.wait_ge(s["v_mm"], U * i + u + 1)
                for e in range(2):
                    ins = nc.vector.tensor_tensor(
                        vpad[0:t, u, :, e, e, :],
                        bank[b][0:t, 0:E].rearrange("p (j e d) -> p j e d", e=2, d=DH)[:, :, e, :],
                        bv[0:t, :].rearrange("p (j e d) -> p j e d", e=2, d=DH)[:, :, e, :], ALU.add)
                ins.then_inc(s["vpad_ready"], 1)

            def f_cum(i, ft):
                dve.wait_ge(s["kT_ready"], KT * i + ft + 1)
                nc.vector.tensor_tensor_scan(kcum[:, ft, :], restart[:, :], kT[:, ft, :], 0.0,
                                             ALU.mult, ALU.add).then_inc(s["kcum_ready"], 1)

            def f_sc(i, ju):
                u = ju // KT
                t = T[u]
                for half in range(2):
                    j = 2 * ju + half
                    j4 = j - 4 * u
                    dve.wait_ge(s["s_mm"], 12 * i + j + 1)
                    nc.vector.tensor_tensor(
                        S[0:t, u, 4 * j4:4 * j4 + 4, 0:t],
                        bank[S_BANK[j % 2]][0:t, 0:4 * t].rearrange("p (h t) -> p h t", h=4),
                        mask01[0:t, 0:t].rearrange("p (o t) -> p o t", o=1).to_broadcast([t, 4, t]),
                        ALU.mult).then_inc(s["s_masked"], 1)

            def f_fl(i, ft):
                dve.wait_ge(s["den_mm"], KT * i + ft + 1)
                nc.vector.tensor_scalar(rden[:, ft, :], bank[DEN_BANK[ft]][:, 0:STOK], DEN_EPS, None,
                                        ALU.max).then_inc(s["den_floor"], 1)

            def f_rc(i, ft):
                dve.wait_ge(s["den_floor"], KT * i + ft + 1)
                nc.vector.reciprocal(rden[:, ft, :], rden[:, ft, :]).then_inc(s["rden_ready"], 1)

            def f_av(i, u):
                o, t = OFF[u], T[u]
                dve.wait_ge(s["rden_ready"], KT * i + KT)
                dve.wait_ge(s["av_mm"], U * i + u + 1)
                nc.vector.tensor_tensor(attnT[:, u, :, 0:t],
                                        bank[AV_BANK][:, 0:KT * t].rearrange("p (k t) -> p k t", k=KT),
                                        rden[:, :, o:o + t], ALU.mult).then_inc(s["attnT_ready"], 1)

            def f_wo(i, u):
                t = T[u]
                dve.wait_ge(s["wo_mm"], U * i + u + 1)
                dve.wait_ge(s["hbo_ready"], U * i + u + 1)
                if not (isinstance(i, int) and i == 0):
                    dve.wait_ge(s["out_ready"], U * (i - 1) + u + 1)
                nc.vector.tensor_tensor(hB[0:t, u, :], bank[WO_BANK][0:t, 0:E], hbo[0:t, u, :],
                                        ALU.add).then_inc(s["h1_ready"], 1)

            def b_ffn(i, u):
                t, b, c = T[u], FB + u, U * i + u + 1
                dve.wait_ge(s["ffn_mm"], c)
                nc.vector.tensor_tensor(logit[0:t, u, :], bank[b][0:t, E:E + NE], routb[0:t, :],
                                        ALU.add).then_inc(s["logit_ready"], 1)
                nc.vector.tensor_scalar(mid[0:t, u, :], bank[b][0:t, E + NE:NCAT], LORA_SCALING, None,
                                        ALU.mult).then_inc(s["mid_ready"], 1)

            def b_lmax(i, u):
                t, c = T[u], U * i + u + 1
                dve.wait_ge(s["logit_ready"], c)
                nc.vector.tensor_reduce(lmax[0:t, u:u + 1], logit[0:t, u, :], AX, ALU.max
                                        ).then_inc(s["lmax_ready"], 1)

            def b_lsub(i, u):
                t, c = T[u], U * i + u + 1
                dve.wait_ge(s["lmax_ready"], c)
                nc.vector.tensor_scalar(lsub[0:t, u, :], logit[0:t, u, :], lmax[0:t, u:u + 1], None,
                                        ALU.subtract).then_inc(s["lsub_ready"], 1)

            def b_h2a(i, u):
                t, b, c = T[u], FB + u, U * i + u + 1
                dve.wait_ge(s["hbb_ready"], c)
                dve.wait_ge(s["ffn_mm"], c)
                nc.vector.tensor_tensor(hB[0:t, u, :], bank[b][0:t, 0:E], hbb[0:t, u, :],
                                        ALU.add).then_inc(s["h2a_ready"], 1)

            def b_lrec(i, u):
                t, c = T[u], U * i + u + 1
                dve.wait_ge(s["lexp_ready"], c)
                nc.vector.reciprocal(lrec[0:t, u:u + 1], lsum[0:t, u:u + 1]).then_inc(s["lrec_ready"], 1)

            def b_gate(i, u):
                t, c = T[u], U * i + u + 1
                dve.wait_ge(s["lrec_ready"], c)
                nc.vector.tensor_scalar(gate[0:t, u, :], lexp[0:t, u, :], lrec[0:t, u:u + 1], None,
                                        ALU.mult).then_inc(s["gate_ready"], 1)

            def b_z(i, u):
                t, c = T[u], U * i + u + 1
                dve.wait_ge(s["gate_ready"], c)
                dve.wait_ge(s["mid_ready"], c)
                nc.vector.tensor_tensor(
                    z[0:t, u, 0:NE * R].rearrange("p (e r) -> p e r", e=NE),
                    gate[0:t, u, :].rearrange("p (e o) -> p e o", o=1).to_broadcast([t, NE, R]),
                    mid[0:t, u:u + 1, :].to_broadcast([t, NE, R]), ALU.mult).then_inc(s["z_ready"], 1)

            def b_lora(i, u):
                t, c = T[u], U * i + u + 1
                dve.wait_ge(s["lora_mm"], c)
                dve.wait_ge(s["h2a_ready"], c)
                nc.vector.tensor_tensor(hB[0:t, u, :], bank[FB + u][0:t, 0:E], hB[0:t, u, :],
                                        ALU.add).then_inc(s["h2_ready"], 1)

            def b_sc(i, u):
                t, c = T[u], U * i + u + 1
                dve.wait_ge(s["sc_mm"], c)
                nc.vector.tensor_tensor(sm[0:t, u, 0:t], bank[FB + u][0:t, 0:t], maskadd[0:t, 0:t],
                                        ALU.add).then_inc(s["sm_ready"], 1)

            def b_smax(i, u):
                t, c = T[u], U * i + u + 1
                dve.wait_ge(s["sm_ready"], c)
                nc.vector.tensor_reduce(smax[0:t, u:u + 1], sm[0:t, u, 0:t], AX, ALU.max
                                        ).then_inc(s["smax_ready"], 1)

            def b_nmax(i, u):
                t, c = T[u], U * i + u + 1
                dve.wait_ge(s["smax_ready"], c)
                nc.vector.tensor_scalar(nmax[0:t, u:u + 1], smax[0:t, u:u + 1], -float(E) ** -0.5, None,
                                        ALU.mult).then_inc(s["nmax_ready"], 1)

            def b_prec(i, u):
                t, c = T[u], U * i + u + 1
                dve.wait_ge(s["prob_ready"], c)
                nc.vector.reciprocal(prec[0:t, u:u + 1], psm[0:t, u:u + 1]).then_inc(s["prec_ready"], 1)

            def b_pv(i, u):
                t, c = T[u], U * i + u + 1
                dve.wait_ge(s["prec_ready"], c)
                dve.wait_ge(s["pv_mm"], c)
                nc.vector.scalar_tensor_tensor(out=hB[0:t, u, :], in0=bank[FB + u][0:t, 0:E],
                                               scalar=prec[0:t, u:u + 1], in1=hB[0:t, u, :],
                                               op0=ALU.mult, op1=ALU.add).then_inc(s["h3_ready"], 1)

            def mix(name, dst, mu):
                def step(i, u):
                    n = IMGS[u]
                    dve.wait_ge(s["xd_ready"], U * i + u + 1)
                    for k in range(KT):
                        ins = nc.vector.scalar_tensor_tensor(
                            out=dst[:, u, k, 0:T[u]].rearrange("p (b t) -> p b t", b=n),
                            in0=xd[:, u, k, 0:T[u]].rearrange("p (b t) -> p b t", b=n), scalar=mu[:, k:k + 1],
                            in1=xs[:, u, k, 0:n, 0:NTOK], op0=ALU.mult, op1=ALU.add)
                    ins.then_inc(s[name], 1)
                return step

            def b_rkv(i, u):
                t, c = T[u], U * i + u + 1
                dve.wait_ge(s["kv_mm"], c)
                dve.wait_ge(s["rt_ready"], c)
                nc.vector.scalar_tensor_tensor(out=rkv[0:t, u, :], in0=rt[0:t, u, :], scalar=1.0,
                                               in1=bank[FB + u][0:t, 0:E], op0=ALU.add, op1=ALU.mult
                                               ).then_inc(s["rkv_ready"], 1)

            run(dve, {"P_tok": f_tok, "P_lo": f_tr, "F_v": f_v, "F_k": feature_k, "F_cum": f_cum,
                      "F_q": feature_q, "F_sc": f_sc, "F_fl": f_fl,
                      "F_rc": f_rc, "F_av": f_av, "F_wo": f_wo,
                      "P_st0": stats(0, hF, s["hF_ready"]), "P_mv0": mean_var(0), "P_ve0": var_eps(0),
                      "F_st1": stats(1, hB, s["h1_ready"]), "F_mv1": mean_var(1), "F_ve1": var_eps(1),
                      "B_st2": stats(2, hB, s["h2_ready"]), "B_mv2": mean_var(2), "B_ve2": var_eps(2),
                      "B_st3": stats(3, hB, s["h3_ready"]), "B_mv3": mean_var(3), "B_ve3": var_eps(3),
                      "B_ffn": b_ffn, "B_lmax": b_lmax, "B_lsub": b_lsub, "B_h2a": b_h2a, "B_lrec": b_lrec,
                      "B_gate": b_gate, "B_z": b_z, "B_lora": b_lora, "B_sc": b_sc, "B_smax": b_smax,
                      "B_nmax": b_nmax, "B_prec": b_prec, "B_pv": b_pv, "B_xr": mix("xr_ready", xr, mur),
                      "B_xk": mix("xk_ready", xk, muk), "B_rkv": b_rkv},
                DVE_BODY, {"P_lo0": w_split})


def kernel(**inputs):
    import numpy as _np
    import concourse.bacc as _bacc
    from concourse import mybir as _mybir
    from concourse.bass_utils import run_bass_kernel_spmd as _run

    host = {n: _np.asarray(v) for n, v in inputs.items()}
    x = host["x"].reshape(B, GRID, PATCH, GRID, PATCH, C).transpose(0, 1, 3, 2, 4, 5)
    x = x.reshape(STEPS, STOK, KC, P).transpose(0, 3, 2, 1).reshape(STEPS * P, KC, STOK)
    laid = {"x": x}
    for n in ("L0_tok_W_proj", "L0_attn_Wk", "L0_attn_Wv", "L0_attn_Wq", "L0_attn_Wo", "L1_attn_Qw", "L1_attn_Kw",
              "L1_ffn_W_r", "L1_ffn_W_k", "L1_ffn_W_v"):
        laid[n] = host[n].T
    laid["L0_ffn_cat"] = _np.concatenate([host["L0_ffn_base_w"].T, host["L0_ffn_router_w"].T,
                                          host["L0_ffn_lora_A"]], axis=1)
    laid["L0_ffn_lora_B"] = host["L0_ffn_lora_B"].reshape(NE * R, E)
    for n in ("L1_attn_Vw", "L0_tok_b_proj", "L0_tok_pos_emb", "L0_attn_bq", "L0_attn_bk", "L0_attn_bv", "L0_attn_bo",
              "L0_ffn_base_b", "L0_ffn_router_b", "L1_ffn_mu_r", "L1_ffn_mu_k"):
        laid[n] = host[n]

    nc = _bacc.Bacc("TRN2", target_bir_lowering=False, num_devices=1)
    arrays, args = {}, {}
    for name, v in laid.items():
        v = _np.ascontiguousarray(v)
        arrays[f"in_{name}_dram"] = v
        args[name] = nc.dram_tensor(f"in_{name}_dram", v.shape, _mybir.dt.from_np(v.dtype), kind="ExternalInput").ap()
    args["out"] = nc.dram_tensor("out_0_dram", (B, NTOK, E), F32, kind="ExternalOutput").ap()
    vit_tower_kernel(nc, args)
    r = _run(nc, [arrays], core_ids=[0])
    return r.results[0]["out_0_dram"]
```
